# Optimizing a Trainium2 kernel written in Bass

```python
import numpy as np
import jax
import jax.numpy as jnp

def _softmax(x, axis=-1):
    return jax.nn.softmax(x, axis=axis)

def _gelu(x):
    return jax.nn.gelu(x, approximate=True)

def _silu(x):
    return jax.nn.silu(x)

def _sigmoid(x):
    return jax.nn.sigmoid(x)

def _layernorm(x, axis=-1, eps=1e-05):
    m = jnp.mean(x, axis=axis, keepdims=True)
    v = jnp.var(x, axis=axis, keepdims=True)
    return (x - m) / jnp.sqrt(v + eps)

def _scatter_add(tgt, idx, src, axis=0):
    return tgt.at[idx].add(src)

def _segment_sum(src, seg, n):
    return jax.ops.segment_sum(src, seg, n)
kernel_name = 'mk_sandwich_d1_jaxref_r4_a2945f'

def setup_inputs(seed: int=0):
    np.random.seed(seed)
    _w = jnp.asarray

    def _L0_attn_setup():
        import jax, jax.numpy as jnp
        import numpy as np
        CHUNK = 64
        NORM_EPS = 1e-05
        DENOM_EPS = 1.0
        B, S, HID, H = (4, 1024, 256, 8)
        D = HID // H

        def rmsnorm(x, w, eps=NORM_EPS):
            var = jnp.mean(x * x, axis=-1, keepdims=True)
            return x * jax.lax.rsqrt(var + eps) * w

        def chunked_linear_attn(q, k, v):
            b, s, h, d = q.shape
            n = s // CHUNK

            def to_chunks(x):
                return x.reshape(b, n, CHUNK, h, d).transpose(1, 0, 3, 2, 4)
            qc, kc, vc = (to_chunks(q), to_chunks(k), to_chunks(v))
            mask = jnp.tril(jnp.ones((CHUNK, CHUNK), dtype=q.dtype))

            def step(state, inp):
                qq, kk, vv = inp
                inter = jnp.einsum('bhcd,bhde->bhce', qq, state)
                scores = jnp.einsum('bhcd,bhed->bhce', qq, kk) * mask
                intra = jnp.einsum('bhce,bhed->bhcd', scores, vv)
                state = state + jnp.einsum('bhcd,bhce->bhde', kk, vv)
                return (state, inter + intra)
            init = jnp.zeros((b, h, d, d), dtype=q.dtype)
            _, o = jax.lax.scan(step, init, (qc, kc, vc))
            return o.transpose(1, 0, 3, 2, 4).reshape(b, s, h, d)
        key = jax.random.key(seed)
        k0, k1, k2, k3, k4 = jax.random.split(key, 5)
        hidden_states = jax.random.normal(k0, (B, S, HID), dtype=jnp.float32)
        Wq = jax.random.normal(k1, (HID, HID), dtype=jnp.float32) * 0.02
        Wk = jax.random.normal(k2, (HID, HID), dtype=jnp.float32) * 0.02
        Wv = jax.random.normal(k3, (HID, HID), dtype=jnp.float32) * 0.02
        Wo = jax.random.normal(k4, (HID, HID), dtype=jnp.float32) * 0.02
        norm_w = jnp.ones((D,), dtype=jnp.float32)
        return {'hidden_states': hidden_states, 'Wq': Wq, 'Wk': Wk, 'Wv': Wv, 'Wo': Wo, 'norm_w': norm_w}
    _L0_attn_in = _L0_attn_setup()

    def _L0_ffn_setup():
        import jax, jax.numpy as jnp
        import numpy as np
        import math
        GOLDEN_CENTER = 1.0 / math.e
        GOLDEN_LOWER = 0.5 - math.log(4.0 / 3.0)
        GOLDEN_UPPER = 0.5
        B, T, D = (4, 512, 256)
        E = 8
        I = 1024 // (E // 2)

        def _routing_weights(x, Wr, temperature):
            inh = jax.nn.sigmoid(x @ Wr / temperature)
            in_zone = (inh >= GOLDEN_LOWER) & (inh <= GOLDEN_UPPER)
            dist = jnp.abs(inh - GOLDEN_CENTER)
            w = jnp.exp(-dist / 0.1) * in_zone.astype(x.dtype)
            wsum = w.sum(axis=-1, keepdims=True)
            no_expert = wsum < 1e-08
            fb = jnp.exp(-dist / 0.3)
            _, top2 = jax.lax.top_k(fb, 2)
            fb_mask = jax.nn.one_hot(top2, E, dtype=x.dtype).sum(axis=-2)
            fb_w = fb * fb_mask
            fb_w = fb_w / jnp.clip(fb_w.sum(axis=-1, keepdims=True), 1e-08)
            w = jnp.where(no_expert, fb_w, w)
            wsum = w.sum(axis=-1, keepdims=True)
            return w / jnp.clip(wsum, 1e-08)
        key = jax.random.key(seed)
        k = jax.random.split(key, 6)
        s_d = 1.0 / math.sqrt(D)
        s_i = 1.0 / math.sqrt(I)
        return {'x': jax.random.normal(k[0], (B, T, D), jnp.float32), 'Wg': jax.random.normal(k[1], (E, D, I), jnp.float32) * s_d, 'Wu': jax.random.normal(k[2], (E, D, I), jnp.float32) * s_d, 'Wd': jax.random.normal(k[3], (E, I, D), jnp.float32) * s_i, 'Wr': jax.random.normal(k[4], (D, E), jnp.float32) * s_d, 'temperature': jnp.ones((1,), jnp.float32)}
    _L0_ffn_in = _L0_ffn_setup()
    _d = {'L0_attn_hidden_states': _L0_attn_in['hidden_states'], 'L0_attn_Wq': _L0_attn_in['Wq'], 'L0_attn_Wk': _L0_attn_in['Wk'], 'L0_attn_Wv': _L0_attn_in['Wv'], 'L0_attn_Wo': _L0_attn_in['Wo'], 'L0_attn_norm_w': _L0_attn_in['norm_w'], 'L0_ffn_Wg': _L0_ffn_in['Wg'], 'L0_ffn_Wu': _L0_ffn_in['Wu'], 'L0_ffn_Wd': _L0_ffn_in['Wd'], 'L0_ffn_Wr': _L0_ffn_in['Wr'], 'L0_ffn_temperature': _L0_ffn_in['temperature']}
    _x0 = _d['L0_attn_hidden_states']
    _d['L0_attn_hidden_states'] = jax.random.normal(jax.random.fold_in(jax.random.key(seed), 1), (2, 4096, 256), dtype=_x0.dtype)
    del _x0
    return _d

def reference(L0_attn_hidden_states, L0_attn_Wq, L0_attn_Wk, L0_attn_Wv, L0_attn_Wo, L0_attn_norm_w, L0_ffn_Wg, L0_ffn_Wu, L0_ffn_Wd, L0_ffn_Wr, L0_ffn_temperature):

    def _L0_attn_ref(hidden_states, Wq, Wk, Wv, Wo, norm_w):
        import jax, jax.numpy as jnp
        import numpy as np
        CHUNK = 64
        NORM_EPS = 1e-05
        DENOM_EPS = 1.0
        B, S, HID, H = (4, 1024, 256, 8)
        D = HID // H

        def rmsnorm(x, w, eps=NORM_EPS):
            var = jnp.mean(x * x, axis=-1, keepdims=True)
            return x * jax.lax.rsqrt(var + eps) * w

        def chunked_linear_attn(q, k, v):
            b, s, h, d = q.shape
            n = s // CHUNK

            def to_chunks(x):
                return x.reshape(b, n, CHUNK, h, d).transpose(1, 0, 3, 2, 4)
            qc, kc, vc = (to_chunks(q), to_chunks(k), to_chunks(v))
            mask = jnp.tril(jnp.ones((CHUNK, CHUNK), dtype=q.dtype))

            def step(state, inp):
                qq, kk, vv = inp
                inter = jnp.einsum('bhcd,bhde->bhce', qq, state)
                scores = jnp.einsum('bhcd,bhed->bhce', qq, kk) * mask
                intra = jnp.einsum('bhce,bhed->bhcd', scores, vv)
                state = state + jnp.einsum('bhcd,bhce->bhde', kk, vv)
                return (state, inter + intra)
            init = jnp.zeros((b, h, d, d), dtype=q.dtype)
            _, o = jax.lax.scan(step, init, (qc, kc, vc))
            return o.transpose(1, 0, 3, 2, 4).reshape(b, s, h, d)
        b, s, _ = hidden_states.shape
        q = jnp.einsum('bsd,ed->bse', hidden_states, Wq).reshape(b, s, H, D)
        k = jnp.einsum('bsd,ed->bse', hidden_states, Wk).reshape(b, s, H, D)
        v = jnp.einsum('bsd,ed->bse', hidden_states, Wv).reshape(b, s, H, D)
        o = chunked_linear_attn(q, k, v)
        z = jnp.cumsum(k, axis=1)
        denom = jnp.maximum(jnp.abs(jnp.sum(q * z, axis=-1)), DENOM_EPS)[..., None]
        o = o / denom
        o = rmsnorm(o, norm_w)
        o = o.reshape(b, s, H * D)
        return jnp.einsum('bse,de->bsd', o, Wo)

    def _L0_ffn_ref(x, Wg, Wu, Wd, Wr, temperature):
        import jax, jax.numpy as jnp
        import numpy as np
        import math
        GOLDEN_CENTER = 1.0 / math.e
        GOLDEN_LOWER = 0.5 - math.log(4.0 / 3.0)
        GOLDEN_UPPER = 0.5
        B, T, D = (4, 512, 256)
        E = 8
        I = 1024 // (E // 2)

        def _routing_weights(x, Wr, temperature):
            inh = jax.nn.sigmoid(x @ Wr / temperature)
            in_zone = (inh >= GOLDEN_LOWER) & (inh <= GOLDEN_UPPER)
            dist = jnp.abs(inh - GOLDEN_CENTER)
            w = jnp.exp(-dist / 0.1) * in_zone.astype(x.dtype)
            wsum = w.sum(axis=-1, keepdims=True)
            no_expert = wsum < 1e-08
            fb = jnp.exp(-dist / 0.3)
            _, top2 = jax.lax.top_k(fb, 2)
            fb_mask = jax.nn.one_hot(top2, E, dtype=x.dtype).sum(axis=-2)
            fb_w = fb * fb_mask
            fb_w = fb_w / jnp.clip(fb_w.sum(axis=-1, keepdims=True), 1e-08)
            w = jnp.where(no_expert, fb_w, w)
            wsum = w.sum(axis=-1, keepdims=True)
            return w / jnp.clip(wsum, 1e-08)
        weights = _routing_weights(x, Wr, temperature)
        gate = jnp.einsum('btd,edi->beti', x, Wg)
        up = jnp.einsum('btd,edi->beti', x, Wu)
        h = jax.nn.silu(gate) * up
        e_out = jnp.einsum('beti,eid->betd', h, Wd)
        out = jnp.einsum('bte,betd->btd', weights, e_out)
        return out
    x = L0_attn_hidden_states
    x = x + _layernorm(_L0_attn_ref(_layernorm(x, axis=-1), L0_attn_Wq, L0_attn_Wk, L0_attn_Wv, L0_attn_Wo, L0_attn_norm_w), axis=-1)
    x = x + _layernorm(_L0_ffn_ref(_layernorm(x, axis=-1), L0_ffn_Wg, L0_ffn_Wu, L0_ffn_Wd, L0_ffn_Wr, L0_ffn_temperature), axis=-1)
    return x

_drawn_inputs = setup_inputs


def setup_inputs(seed=0):
    import zlib

    import numpy as np

    out = dict(_drawn_inputs(seed))
    spreads = {'L0_attn_norm_w': (1.0, 0.2)}
    factors = {}
    for name, (base, spread) in spreads.items():
        noise = np.random.default_rng([zlib.crc32(name.encode()), seed]).standard_normal(out[name].shape)
        drawn = base * np.exp(spread * noise) if base else spread * noise
        out[name] = jnp.asarray(drawn.astype(out[name].dtype))
    for name, factor in factors.items():
        out[name] = (out[name] * factor).astype(out[name].dtype)
    return out
```

```python
import math
from contextlib import ExitStack

import concourse.bass as bass
from concourse import mybir

B, S, HID = 2, 4096, 256
H, D = 8, 32
E, INNER = 8, 256
P = 128
KT = HID // P
HG = H * D // P
HPG = H // HG
MT = INNER // P
CHUNK = P
ROWS = 256
BLOCKS = S // ROWS
TILES = B * ROWS // P
TOK = TILES * P
VA = D + 1
GV = HPG * VA

LN_EPS = 1e-5
RMS_EPS = 1e-5
DENOM_EPS = 1.0
CENTER = 1.0 / math.e
LOWER = 0.5 - math.log(4.0 / 3.0)
UPPER = 0.5
TINY = 1e-8

STEPS = [
    [("ln1_stats",)],
    [("ln1_apply",)],
    [("xt", 0), ("xt", 1)],
    [("kv", 0), ("q", 0)],
    [("q", 1), ("kt", 0), ("keep_x1",)],
    [("kv", 1), ("s", 0, 0)],
    [("s", 0, 1), ("kt", 1)],
    [("o", 0), ("su", 0)],
    [("s", 1, 0), ("kv", 2)],
    [("s", 1, 1), ("norm_stats", 0)],
    [("o", 1), ("su", 1), ("kt", 2), ("norm_apply", 0)],
    [("s", 2, 0), ("ot", 0)],
    [("s", 2, 1), ("norm_stats", 1), ("kv", 3)],
    [("o", 2), ("su", 2), ("kt", 3), ("norm_apply", 1)],
    [("s", 3, 0), ("ot", 1)],
    [("s", 3, 1), ("norm_stats", 2), ("wo", 0)],
    [("o", 3), ("su", 3), ("norm_apply", 2), ("ln2_stats", 0)],
    [("norm_stats", 3), ("ot", 2), ("ln2_apply", 0)],
    [("norm_apply", 3), ("ln3_stats", 0)],
    [("ot", 3), ("ln3_apply", 0)],
    [("wo", 1)],
    [("ln2_stats", 1)],
    [("ln2_apply", 1), ("ln3_stats", 1)],
    [("ln3_apply", 1)],
    [("ft", 0)],
    [("ft", 1), ("ft_out", 0), ("ft_out", 1)],
    [],
    [],
]
ROUTER = ("r",)
PSUM_STEPS = [s for after in STEPS for s in after if s[0] in ("xt", "q", "kv", "kt", "s", "o", "su", "ot", "wo", "ft")]
PSUM_STEPS.append(ROUTER)
NUMBER = {s: n for n, s in enumerate(PSUM_STEPS)}
N_PSUM = len(PSUM_STEPS)


def build_program(nc, x, wq_t, wkv_t, wo_t, norm_w, wg, wu, wd, wr, temperature, out):
    f32, f32r = mybir.dt.float32, mybir.dt.float32r
    ALU, ACT, AX = mybir.AluOpType, mybir.ActivationFunctionType, mybir.AxisListType

    ctx = ExitStack()
    with ctx:
        def sb(name, shape, dt=f32):
            return ctx.enter_context(nc.sbuf_tensor(name, shape, dt))

        def sem(name):
            return ctx.enter_context(nc.semaphore(name))

        w_hi = sb("w_hi", [P, 3 * E, 2, 256], f32r)
        w_lo = sb("w_lo", [P, 3 * E, 2, 256], f32r)
        wq_hi, wq_lo = sb("wq_hi", [P, KT, HID], f32r), sb("wq_lo", [P, KT, HID], f32r)
        wkv_hi, wkv_lo = sb("wkv_hi", [P, KT, 2 * HID], f32r), sb("wkv_lo", [P, KT, 2 * HID], f32r)
        wo_hi, wo_lo = sb("wo_hi", [P, HG, HID], f32r), sb("wo_lo", [P, HG, HID], f32r)
        wr_raw = sb("wr_raw", [P, KT, E])
        wr_hl = sb("wr_hl", [P, KT, 2 * E], f32r)
        wr_h0 = sb("wr_h0", [P, KT, 2 * E], f32r)
        nw = sb("nw", [P, HG])
        temp = sb("temp", [P, 1])
        half_inv_t = sb("half_inv_t", [P, 1])

        xs = sb("xs", [P, TILES, HID])
        rows = sb("rows", [P, TILES, HID])
        xt_hi, xt_lo = sb("xt_hi", [P, KT, TOK], f32r), sb("xt_lo", [P, KT, TOK], f32r)
        q_t = sb("q_t", [P, HG, TOK])
        k_sb = sb("k_sb", [P, TILES, H * D])
        v_sb = sb("v_sb", [P, TILES, H, VA])
        kz = sb("kz", [P, HG, HPG, P])
        prob = sb("prob", [P, H, P])
        state = sb("state", [P, B, HG, GV])
        state_add = sb("state_add", [P, HG, GV])
        o_sb = sb("o_sb", [P, 2, H, VA])
        o_sq = sb("o_sq", [P, H, VA])
        o_n = sb("o_n", [P, 2, H, D])
        ot_hi, ot_lo = (xt[:, 0, :].rearrange("p (a g n) -> p a g n", a=2, g=HG) for xt in (xt_hi, xt_lo))
        x1 = sb("x1", [P, TILES, HID])

        ft_hi, ft_lo = sb("ft_hi", [P, KT, TOK], f32r), sb("ft_lo", [P, KT, TOK], f32r)
        h_hi, h_lo = sb("h_hi", [P, 2, MT, TOK], f32r), sb("h_lo", [P, 2, MT, TOK], f32r)
        NSTAGE = 6
        late = sb("late", [P, NSTAGE * 512])
        h_f = late[:, 0:1024].rearrange("p (m n) -> p m n", m=MT)
        acc = late[:, 1024:2048].rearrange("p (t n) -> p t n", t=TILES)
        x1_kept = late[:, 2048:3072].rearrange("p (t n) -> p t n", t=TILES)

        bn1, bn2, bn3, bn4 = (sb(f"bn{n}", [P, TILES, 6]) for n in (1, 2, 3, 4))
        mv1, mv2, mv3, mv4 = (sb(f"mv{n}", [P, TILES, 2]) for n in (1, 2, 3, 4))
        var1, var2, var3, var4 = (sb(f"var{n}", [P, TILES]) for n in (1, 2, 3, 4))
        rstd1, rstd2, rstd3, rstd4 = (sb(f"rstd{n}", [P, TILES]) for n in (1, 2, 3, 4))
        den2, ssq = sb("den2", [P, H]), sb("ssq", [P, H])
        rms_in, rms_f = sb("rms_in", [P, H]), sb("rms_f", [P, 2, H])
        ident = sb("ident", [P, P])
        causal = sb("causal", [P, 1, P])
        diag = sb("diag", [P, 1, HPG, VA])
        before = sb("before", [P, 1, E, E])
        minus_half, minus_one = sb("minus_half", [P, H]), sb("minus_one", [P, TILES])
        euler = sb("euler", [P, TILES, E])
        rz = sb("rz", [P, TILES, 2, E])
        logit, tanh, inh = (sb(n, [P, TILES, E]) for n in ("logit", "tanh", "inh"))
        off, neg_off, dist, zone, zone2 = (sb(n, [P, TILES, E]) for n in ("off", "neg_off", "dist", "zone", "zone2"))
        expo, fallback, cube, rank = (sb(n, [P, TILES, E]) for n in ("expo", "fallback", "cube", "rank"))
        nearer, as_near = sb("nearer", [P, TILES, E, E]), sb("as_near", [P, TILES, E, E])
        kinds = sb("kinds", [P, 2, TILES, E])
        sums, guarded, chosen = (sb(n, [P, 2, TILES]) for n in ("sums", "guarded", "chosen"))
        route = sb("route", [P, TILES, E])

        def bank(name):
            return ctx.enter_context(nc.psum_tensor(name, [P, 512], f32))

        gate_ps = [bank(f"gate_ps{m}") for m in range(MT)]
        up_ps = [bank(f"up_ps{m}") for m in range(MT)]
        down_ps = [bank(f"down_ps{p}") for p in range(2)]
        att_ps = [bank(f"att_ps{n}") for n in range(2)]

        def counter(name, per_block, before_first=0):
            return sem(name), per_block, before_first

        x_loaded = counter("x_loaded", 32)
        out_stored = counter("out_stored", 32, 32)
        att_done = counter("att_done", N_PSUM)
        xn_ready = counter("xn_ready", 1)
        xt_hi_ready = counter("xt_hi_ready", KT)
        xt_ready = counter("xt_ready", KT)
        q_ready = counter("q_ready", HG)
        k_ready = counter("k_ready", TILES)
        v_ready = counter("v_ready", TILES)
        kz_ready = counter("kz_ready", TILES)
        prob_ready = counter("prob_ready", TILES * HG)
        o_copied = counter("o_copied", TILES)
        o_squared = counter("o_squared", TILES)
        rms_in_ready = counter("rms_in_ready", TILES)
        rms_ready = counter("rms_ready", TILES)
        on_ready = counter("on_ready", TILES)
        su_read = counter("su_read", TILES)
        state_ready = counter("state_ready", TILES)
        ot_hi_ready = counter("ot_hi_ready", TILES)
        ot_ready = counter("ot_ready", TILES)
        wo_copied = counter("wo_copied", 2)
        x1_ready = counter("x1_ready", 2)
        x1n_ready = counter("x1n_ready", 2)
        x1_copied = counter("x1_copied", 1)
        ft_hi_ready = counter("ft_hi_ready", 2)
        ft_ready = counter("ft_ready", 2)
        var_ready = [counter(f"var{n}_ready", k) for n, k in ((1, 1), (2, 2), (3, 2), (4, 1))]
        rstd_ready = [counter(f"rstd{n}_ready", k) for n, k in ((1, 1), (2, 2), (3, 2), (4, 1))]
        rz_copied = counter("rz_copied", 1)
        logit_ready = counter("logit_ready", 1)
        tanh_ready = counter("tanh_ready", 1)
        dist_ready = counter("dist_ready", 1)
        fallback_ready = counter("fallback_ready", 1)
        rank_ready = counter("rank_ready", 1)
        route_ready = counter("route_ready", 1)
        up_done = counter("up_done", 2 * E)
        silu_ready = counter("silu_ready", 2 * E)
        h_ready = counter("h_ready", 2 * E)
        h_hi_ready = counter("h_hi_ready", 2 * E)
        h_lo_ready = counter("h_lo_ready", 2 * E)
        down_done = counter("down_done", 2 * E, 2)
        down_read = counter("down_read", 2 * E, 2)
        out_ready = counter("out_ready", 1)
        att_w_loaded = [sem(f"att_w_loaded{n}") for n in range(3)]
        small_loaded = sem("small_loaded")
        stage_loaded = [sem(f"stage_loaded{n}") for n in range(NSTAGE)]
        w_hi_ready = sem("w_hi_ready")
        w_ready = sem("w_ready")
        wo_scaled = sem("wo_scaled")
        wr_hi_ready = sem("wr_hi_ready")
        wr_ready = sem("wr_ready")
        temp_ready = sem("temp_ready")
        const_ready = sem("const_ready")
        dve_own, pool_own = sem("dve_own"), sem("pool_own")

        def reach(eng, count, block, k):
            s, per_block, first = count
            base, offset = block
            value = offset * per_block + k + first
            if isinstance(base, int):
                if base * per_block + value > first:
                    eng.wait_ge(s, base * per_block + value)
            else:
                eng.wait_ge(s, base * per_block + value)

        READ_OUT = {ROUTER: (rz_copied, 1)}
        for n in range(KT):
            READ_OUT["xt", n] = (xt_ready, n + 1)
        for n in range(HG):
            READ_OUT["q", n] = (q_ready, n + 1)
        for t in range(TILES):
            READ_OUT["kv", t] = (v_ready, t + 1)
            READ_OUT["kt", t] = (kz_ready, t + 1)
            for g in range(HG):
                READ_OUT["s", t, g] = (prob_ready, HG * t + g + 1)
            READ_OUT["o", t] = (o_copied, t + 1)
            READ_OUT["su", t] = (su_read, t + 1)
            READ_OUT["ot", t] = (ot_ready, t + 1)
        for p in range(2):
            READ_OUT["wo", p] = (wo_copied, p + 1)
            READ_OUT["ft", p] = (ft_ready, p + 1)

        def att_bank(step):
            return att_ps[NUMBER[step] % 2]

        UNITS = 3 * E

        def unit_src(u):
            return (wg, wu, wd)[u % 3][u // 3, :, :].rearrange("(k p) n -> p k n", p=P)

        def stage(u):
            n = (u + 4) % NSTAGE
            return n, late[:, 512 * n:512 * n + 512].rearrange("p (k n) -> p k n", k=2)

        wq_raw = late[:, 0:512].rearrange("p (k n) -> p k n", k=KT)
        wkv_raw = late[:, 512:1536].rearrange("p (k n) -> p k n", k=KT)
        wo_raw = late[:, 1536:2048].rearrange("p (k n) -> p k n", k=HG)
        ATT_W = 3

        def rows_of(dram, b, row):
            return dram[b, bass.ds(row, ROWS), :].rearrange("(c p) n -> p c n", p=P)

        def tiles_of(tensor, b):
            return tensor[:, b:TILES:B, :]

        block_scope = ctx.enter_context(nc.Block())

        @block_scope.sync
        def _(sp):
            def load_x(row):
                for b in range(B):
                    sp.dma_start(tiles_of(xs, b), rows_of(x, b, row)).then_inc(x_loaded[0], 16)

            def store_out(block, row):
                reach(sp, out_ready, block, 1)
                for b in range(B):
                    sp.dma_start(rows_of(out, b, row), tiles_of(x1_kept, b)).then_inc(out_stored[0], 16)

            sp.sem_inc(out_stored[0], out_stored[2])
            load_x(0)
            sp.dma_start(wq_raw, wq_t.rearrange("(k p) n -> p k n", p=P)).then_inc(att_w_loaded[0], 16)
            sp.dma_start(wkv_raw, wkv_t.rearrange("(k p) n -> p k n", p=P)).then_inc(att_w_loaded[1], 16)
            sp.dma_start(nw[:, :], norm_w).then_inc(small_loaded, 16)
            sp.dma_start(wr_raw[:, :, :], wr.rearrange("(k p) n -> p k n", p=P)).then_inc(small_loaded, 16)
            sp.dma_start(temp[:, :], temperature.partition_broadcast(P)).then_inc(small_loaded, 16)
            sp.dma_start(wo_raw, wo_t.rearrange("(k p) n -> p k n", p=P)).then_inc(att_w_loaded[2], 16)
            for u in range(UNITS):
                n, slot = stage(u)
                if u >= 2:
                    sp.wait_ge(w_ready, {2: 1, 3: 2, 4: 2, 5: 3}.get(u, ATT_W + u - NSTAGE + 1))
                sp.dma_start(slot, unit_src(u)).then_inc(stage_loaded[n], 16)
            reach(sp, x1_ready, (0, 0), 2)
            load_x(ROWS)
            with sp.Fori(1, BLOCKS - 1) as i:
                reach(sp, x1_ready, (i, 0), 2)
                load_x(i * ROWS + ROWS)
                store_out((i, -1), i * ROWS - ROWS)
            store_out((BLOCKS - 2, 0), (BLOCKS - 2) * ROWS)
            store_out((BLOCKS - 1, 0), (BLOCKS - 1) * ROWS)
            reach(sp, out_stored, (BLOCKS, 0), 0)

        @block_scope.tensor
        def _(pe):
            def products(dst, pairs, start=True, stop=True):
                terms = [t for (l_hi, l_lo), (r_hi, r_lo) in pairs
                         for t in ((l_hi, r_hi), (l_hi, r_lo), (l_lo, r_hi))]
                for n, (lhs, rhs) in enumerate(terms):
                    last = nc.tensor.matmul(dst, lhs, rhs, start=start and n == 0, stop=stop and n == len(terms) - 1)
                return last

            def att_step(step, a):
                if step not in NUMBER:
                    return
                kind, dst, number = step[0], att_bank(step), NUMBER[step]
                before_it = [m for m in range(number) if m % 2 == number % 2]
                if before_it:
                    reach(pe, READ_OUT[PSUM_STEPS[before_it[-1]]][0], a, READ_OUT[PSUM_STEPS[before_it[-1]]][1])
                else:
                    m = max(m for m in range(N_PSUM) if m % 2 == number % 2)
                    count, k = READ_OUT[PSUM_STEPS[m]]
                    reach(pe, count, (a[0], a[1] - 1), k)
                if kind == "xt":
                    k = step[1]
                    reach(pe, xn_ready, a, 1)
                    for t in range(TILES):
                        last = nc.tensor.transpose(dst[:, t * P:t * P + P], rows[:, t, k * P:k * P + P], ident[:, :])
                elif kind == "q":
                    g = step[1]
                    reach(pe, xt_ready, a, KT)
                    last = products(dst[:, :], [((wq_hi[:, k, g * P:g * P + P], wq_lo[:, k, g * P:g * P + P]),
                                                 (xt_hi[:, k, :], xt_lo[:, k, :])) for k in range(KT)])
                elif kind == "kv":
                    t = slice(step[1] * P, step[1] * P + P)
                    reach(pe, xt_ready, a, KT)
                    last = products(dst[:, :], [((xt_hi[:, k, t], xt_lo[:, k, t]), (wkv_hi[:, k, :], wkv_lo[:, k, :]))
                                                for k in range(KT)])
                elif kind == "kt":
                    t = step[1]
                    reach(pe, k_ready, a, t + 1)
                    for g in range(HG):
                        last = nc.tensor.transpose(dst[:, g * P:g * P + P], k_sb[:, t, g * P:g * P + P], ident[:, :])
                elif kind == "s":
                    t, g = step[1:]
                    reach(pe, q_ready, a, g + 1)
                    reach(pe, kz_ready, a, t + 1)
                    for j in range(HPG):
                        last = nc.tensor.matmul(dst[:, j * P:j * P + P], kz[:, g, j, :], q_t[:, g, t * P:t * P + P],
                                                start=True, stop=True)
                elif kind == "o":
                    t = step[1]
                    reach(pe, prob_ready, a, HG * t + HG)
                    reach(pe, v_ready, a, t + 1)
                    reach(pe, state_ready, a, t - B + 1)
                    for g in range(HG):
                        nc.tensor.matmul(dst[:, g * GV:g * GV + GV], q_t[:, g, t * P:t * P + P], state[:, t % B, g, :],
                                         start=True, stop=False)
                        for j in range(HPG):
                            h = g * HPG + j
                            last = nc.tensor.matmul(dst[:, h * VA:h * VA + VA], prob[:, h, :], v_sb[:, t, h, :],
                                                    start=False, stop=j == HPG - 1)
                elif kind == "su":
                    t = step[1]
                    for g in range(HG):
                        last = nc.tensor.matmul(dst[:, g * GV:g * GV + GV], k_sb[:, t, g * P:g * P + P],
                                                v_sb[:, t, g * HPG:g * HPG + HPG, :], start=True, stop=True)
                elif kind == "ot":
                    t = step[1]
                    reach(pe, on_ready, a, t + 1)
                    for g in range(HG):
                        last = nc.tensor.transpose(dst[:, g * P:g * P + P], o_n[:, t % 2, g * HPG:g * HPG + HPG, :],
                                                   ident[:, :])
                elif kind == "wo":
                    p = step[1]
                    reach(pe, ot_ready, a, 2 * p + 2)
                    for t in range(2):
                        last = products(dst[:, t * HID:t * HID + HID],
                                        [((ot_hi[:, t, g, :], ot_lo[:, t, g, :]), (wo_hi[:, g, :], wo_lo[:, g, :]))
                                         for g in range(HG)])
                elif kind == "ft":
                    p = step[1]
                    reach(pe, x1n_ready, a, p + 1)
                    for k in range(KT):
                        for t in range(2):
                            c = (2 * k + t) * P
                            last = nc.tensor.transpose(dst[:, c:c + P], rows[:, 2 * p + t, k * P:k * P + P], ident[:, :])
                elif kind == "r":
                    reach(pe, ft_ready, a, 2)
                    for t in range(TILES):
                        cols, ts = dst[:, t * 2 * E:(t + 1) * 2 * E], slice(t * P, t * P + P)
                        for k in range(KT):
                            nc.tensor.matmul(cols, ft_hi[:, k, ts], wr_hl[:, k, :], start=k == 0, stop=False)
                            last = nc.tensor.matmul(cols, ft_lo[:, k, ts], wr_h0[:, k, :], start=False, stop=k == KT - 1)
                last.then_inc(att_done[0], 1)

            def up(e, m, f):
                reach(pe, ft_ready, f, 2)
                reach(pe, h_ready, f, 2 * e + m - 1)
                c = slice(m * P, m * P + P)
                for n, dst in ((0, gate_ps[m]), (1, up_ps[m])):
                    last = products(dst[:, :], [((w_hi[:, 3 * e + n, k, c], w_lo[:, 3 * e + n, k, c]),
                                                 (ft_hi[:, k, :], ft_lo[:, k, :])) for k in range(KT)])
                last.then_inc(up_done[0], 1)

            def down(e, p, f):
                reach(pe, h_lo_ready, f, 2 * e + 2)
                reach(pe, down_read, f, 2 * e + p - 1)
                for t in range(2):
                    c = slice((2 * p + t) * P, (2 * p + t) * P + P)
                    last = products(down_ps[p][:, t * HID:t * HID + HID],
                                    [((h_hi[:, e % 2, m, c], h_lo[:, e % 2, m, c]),
                                      (w_hi[:, 3 * e + 2, m, :], w_lo[:, 3 * e + 2, m, :])) for m in range(MT)])
                last.then_inc(down_done[0], 1)

            def attention(n, a):
                for step in STEPS[n]:
                    att_step(step, a)

            pe.sem_inc(down_done[0], down_done[2])
            pe.wait_ge(const_ready, 1)
            pe.wait_ge(w_ready, ATT_W)
            for n in range(len(STEPS)):
                attention(n, (0, 0))
            pe.wait_ge(wr_ready, 1)
            att_step(ROUTER, (0, 0))
            pe.wait_ge(w_ready, ATT_W + UNITS)
            up(0, 0, (0, 0))
            up(0, 1, (0, 0))
            with pe.Fori(1, BLOCKS) as i:
                a, f = (i, 0), (i, -1)
                for e in range(1, E - 1):
                    up(e, 0, f)
                    attention(4 * e - 4, a)
                    down(e - 1, 0, f)
                    attention(4 * e - 3, a)
                    up(e, 1, f)
                    attention(4 * e - 2, a)
                    down(e - 1, 1, f)
                    attention(4 * e - 1, a)
                for m in range(MT):
                    up(E - 1, m, f)
                    attention(4 * E - 8 + m, a)
                down(E - 2, 0, f)
                down(E - 2, 1, f)
                att_step(ROUTER, a)
                up(0, 0, a)
                down(E - 1, 0, f)
                up(0, 1, a)
                down(E - 1, 1, f)
            f = (BLOCKS - 1, 0)
            for e in range(1, E):
                up(e, 0, f)
                down(e - 1, 0, f)
                up(e, 1, f)
                down(e - 1, 1, f)
            down(E - 1, 0, f)
            down(E - 1, 1, f)

        @block_scope.scalar
        def _(act):
            def copy(dst, src):
                return nc.scalar.activation(dst, src, ACT.Copy)

            def att_step(step, a):
                kind = step[0]
                if step in NUMBER and kind not in ("s", "su", "ft"):
                    reach(act, att_done, a, NUMBER[step] + 1)
                    src = att_bank(step)
                if kind == "xt":
                    copy(xt_hi[:, step[1], :], src[:, :]).then_inc(xt_hi_ready[0], 1)
                elif kind == "q":
                    copy(q_t[:, step[1], :], src[:, :]).then_inc(q_ready[0], 1)
                elif kind == "kv":
                    t = step[1]
                    copy(k_sb[:, t, :], src[:, 0:HID]).then_inc(k_ready[0], 1)
                    copy(v_sb[:, t, :, 0:D], src[:, HID:2 * HID].rearrange("p (h d) -> p h d", h=H))\
                        .then_inc(v_ready[0], 1)
                elif kind == "kt":
                    for j in range(HPG):
                        r = slice(j * D, j * D + D)
                        last = copy(kz[r, :, j, :], src[r, 0:HG * P].rearrange("p (g s) -> p g s", g=HG))
                    last.then_inc(kz_ready[0], 1)
                elif kind == "o":
                    t = step[1]
                    reach(act, on_ready, a, t - 1)
                    copy(o_sb[:, t % 2, :, :], src[:, 0:H * VA].rearrange("p (h v) -> p h v", h=H))\
                        .then_inc(o_copied[0], 1)
                    reach(act, rms_in_ready, a, t)
                    reach(act, o_copied, a, t + 1)
                    nc.scalar.activation(o_sq[:, :, :], o_sb[:, t % 2, :, :], ACT.Square).then_inc(o_squared[0], 1)
                elif kind == "ot":
                    t = step[1]
                    copy(ot_hi[:, t % 2, :, :], src[:, 0:HG * P].rearrange("p (g n) -> p g n", g=HG))\
                        .then_inc(ot_hi_ready[0], 1)
                elif kind == "wo":
                    p = step[1]
                    copy(rows[:, 2 * p:2 * p + 2, :], src[:, :].rearrange("p (t n) -> p t n", t=2))\
                        .then_inc(wo_copied[0], 1)
                elif kind == "ft_out":
                    p = step[1]
                    reach(act, att_done, a, NUMBER["ft", p] + 1)
                    reach(act, up_done, a, 0)
                    copy(ft_hi[:, :, p * 2 * P:(p + 1) * 2 * P], att_bank(("ft", p))[:, :].rearrange("p (k n) -> p k n", k=KT))\
                        .then_inc(ft_hi_ready[0], 1)
                elif kind == "r":
                    reach(act, logit_ready, a, 0)
                    copy(rz[:, :, :, :], src[:, 0:TILES * 2 * E].rearrange("p (t a e) -> p t a e", t=TILES, a=2))\
                        .then_inc(rz_copied[0], 1)
                    reach(act, logit_ready, a, 1)
                    reach(act, dist_ready, a, 0)
                    nc.scalar.activation(tanh[:, :, :], logit[:, :, :], ACT.Tanh, scale=half_inv_t[:, 0:1])\
                        .then_inc(tanh_ready[0], 1)

            def keep_x1(f):
                reach(act, x1_ready, f, 2)
                reach(act, out_stored, f, 0)
                copy(x1_kept[:, :, :], x1[:, :, :]).then_inc(x1_copied[0], 1)

            def silu(e, m, f):
                reach(act, up_done, f, 2 * e + m + 1)
                reach(act, h_lo_ready, f, 2 * e + m - 1)
                nc.scalar.activation(h_f[:, m, :], gate_ps[m][:, :], ACT.Silu).then_inc(silu_ready[0], 1)

            def high(e, m, f):
                reach(act, h_ready, f, 2 * e + m + 1)
                reach(act, down_done, f, 2 * e - 2)
                copy(h_hi[:, e % 2, m, :], h_f[:, m, :]).then_inc(h_hi_ready[0], 1)

            def attention(n, a, f=None):
                for step in STEPS[n]:
                    if step[0] == "keep_x1":
                        if f is not None:
                            keep_x1(f)
                    else:
                        att_step(step, a)

            def high_of_unit(u):
                n, raw = stage(u)
                act.wait_ge(stage_loaded[n], 16 * ((u // NSTAGE) + 1))
                copy(w_hi[:, u, :, :], raw).then_inc(w_hi_ready, 1)

            act.wait_ge(att_w_loaded[0], 16)
            copy(wq_hi[:, :, :], wq_raw).then_inc(w_hi_ready, 1)
            act.wait_ge(att_w_loaded[1], 16)
            copy(wkv_hi[:, :, :], wkv_raw).then_inc(w_hi_ready, 1)
            act.wait_ge(wo_scaled, 1)
            copy(wo_hi[:, :, :], wo_raw).then_inc(w_hi_ready, 1)
            act.wait_ge(small_loaded, 48)
            copy(wr_hl[:, :, 0:E], wr_raw[:, :, :])
            copy(wr_h0[:, :, 0:E], wr_raw[:, :, :])
            nc.scalar.activation(wr_h0[:, :, E:2 * E], wr_raw[:, :, :], ACT.Copy, scale=0.0).then_inc(wr_hi_ready, 1)
            for n in range(len(STEPS)):
                attention(n, (0, 0))
                if n < UNITS:
                    high_of_unit(n)
            act.wait_ge(temp_ready, 1)
            act.wait_ge(w_ready, ATT_W + UNITS)
            att_step(ROUTER, (0, 0))
            silu(0, 0, (0, 0))
            high(0, 0, (0, 0))
            silu(0, 1, (0, 0))
            high(0, 1, (0, 0))
            with act.Fori(1, BLOCKS) as i:
                a, f = (i, 0), (i, -1)
                for e in range(1, E):
                    for m in range(MT):
                        silu(e, m, f)
                        attention(4 * e - 4 + 2 * m, a, f)
                        high(e, m, f)
                        attention(4 * e - 3 + 2 * m, a, f)
                att_step(ROUTER, a)
                silu(0, 0, a)
                high(0, 0, a)
                silu(0, 1, a)
                high(0, 1, a)
            f = (BLOCKS - 1, 0)
            for e in range(1, E):
                silu(e, 0, f)
                high(e, 0, f)
                silu(e, 1, f)
                high(e, 1, f)
                if e == 1:
                    keep_x1(f)

        @block_scope.vector
        def _(dve):
            def settle(ins):
                ins.then_inc(dve_own, 1)
                dve.wait_ge(dve_own, 1).then_inc(dve_own, -1)

            def low(dst, src, high_part):
                return nc.vector.tensor_tensor(dst, src, high_part.bitcast(f32), ALU.subtract)

            def ln_stats(n, src, tiles, bn, mv, var):
                for t in tiles:
                    last = nc.vector.bn_stats(bn[:, t, :], src[:, t, :])
                settle(last)
                for t in tiles:
                    last = nc.vector.bn_aggr(mv[:, t, :], bn[:, t, :])
                settle(last)
                nc.vector.tensor_scalar(var[:, tiles[0]:tiles[-1] + 1], mv[:, tiles[0]:tiles[-1] + 1, 1], LN_EPS, None,
                                        ALU.add).then_inc(var_ready[n - 1][0], 1)

            def ln_apply(dst, src, tiles, mv, rstd):
                for t in tiles:
                    last = nc.vector.tensor_scalar(dst[:, t, :], src[:, t, :], mv[:, t, 0:1], rstd[:, t:t + 1],
                                                   ALU.subtract, ALU.mult)
                return last

            def att_step(step, a):
                kind = step[0]
                if kind == "ln1_stats":
                    reach(dve, x_loaded, a, 32)
                    ln_stats(1, xs, range(TILES), bn1, mv1, var1)
                elif kind == "ln1_apply":
                    reach(dve, rstd_ready[0], a, 1)
                    ln_apply(rows, xs, range(TILES), mv1, rstd1).then_inc(xn_ready[0], 1)
                elif kind == "xt":
                    k = step[1]
                    reach(dve, xt_hi_ready, a, k + 1)
                    low(xt_lo[:, k, :], att_bank(step)[:, :], xt_hi[:, k, :]).then_inc(xt_ready[0], 1)
                elif kind == "s":
                    t, g = step[1:]
                    reach(dve, att_done, a, NUMBER[step] + 1)
                    nc.vector.tensor_tensor(prob[:, g * HPG:(g + 1) * HPG, :],
                                            att_bank(step)[:, :].rearrange("p (h n) -> p h n", h=HPG),
                                            causal[:, :, :].broadcast_to([P, HPG, P]), ALU.mult)\
                        .then_inc(prob_ready[0], 1)
                elif kind == "su":
                    t = step[1]
                    reach(dve, att_done, a, NUMBER[step] + 1)
                    nc.vector.tensor_tensor(state_add[:, :, :], att_bank(step)[:, 0:HG * GV].rearrange("p (g v) -> p g v", g=HG),
                                            diag[:, :, :, :].rearrange("p a j v -> p a (j v)").broadcast_to([P, HG, GV]),
                                            ALU.mult).then_inc(su_read[0], 1)
                    reach(dve, su_read, a, t + 1)
                    nc.vector.tensor_tensor(state[:, t % B, :, :], state[:, t % B, :, :], state_add[:, :, :], ALU.add)\
                        .then_inc(state_ready[0], 1)
                elif kind == "norm_stats":
                    t = step[1]
                    reach(dve, o_squared, a, t + 1)
                    nc.vector.tensor_scalar(den2[:, :], o_sq[:, :, D], DENOM_EPS ** 2, RMS_EPS, ALU.max, ALU.mult)
                    settle(nc.vector.tensor_reduce(ssq[:, :], o_sq[:, :, 0:D], AX.X, ALU.add))
                    nc.vector.scalar_tensor_tensor(rms_in[:, :], ssq[:, :], 1.0 / D, den2[:, :], ALU.mult, ALU.add)\
                        .then_inc(rms_in_ready[0], 1)
                elif kind == "norm_apply":
                    t = step[1]
                    reach(dve, rms_ready, a, t + 1)
                    if t >= 2:
                        reach(dve, att_done, a, NUMBER["ot", t - 2] + 1)
                    nc.vector.tensor_tensor(o_n[:, t % 2, :, :], o_sb[:, t % 2, :, 0:D],
                                            rms_f[:, t % 2, :].unsqueeze(2).broadcast_to([P, H, D]), ALU.mult)\
                        .then_inc(on_ready[0], 1)
                elif kind == "ot":
                    t = step[1]
                    reach(dve, ot_hi_ready, a, t + 1)
                    low(ot_lo[:, t % 2, :, :], att_bank(step)[:, 0:HG * P].rearrange("p (g n) -> p g n", g=HG),
                        ot_hi[:, t % 2, :, :]).then_inc(ot_ready[0], 1)
                elif kind == "ln2_stats":
                    p = step[1]
                    reach(dve, wo_copied, a, p + 1)
                    ln_stats(2, rows, range(2 * p, 2 * p + 2), bn2, mv2, var2)
                elif kind == "ln2_apply":
                    p = step[1]
                    ts = slice(2 * p, 2 * p + 2)
                    reach(dve, rstd_ready[1], a, p + 1)
                    reach(dve, x1_copied, a, 0)
                    settle(ln_apply(rows, rows, range(2 * p, 2 * p + 2), mv2, rstd2))
                    nc.vector.tensor_tensor(x1[:, ts, :], rows[:, ts, :], xs[:, ts, :], ALU.add).then_inc(x1_ready[0], 1)
                elif kind == "ln3_stats":
                    p = step[1]
                    reach(dve, x1_ready, a, p + 1)
                    ln_stats(3, x1, range(2 * p, 2 * p + 2), bn3, mv3, var3)
                elif kind == "ln3_apply":
                    p = step[1]
                    reach(dve, rstd_ready[2], a, p + 1)
                    ln_apply(rows, x1, range(2 * p, 2 * p + 2), mv3, rstd3).then_inc(x1n_ready[0], 1)
                elif kind == "ft_out":
                    p = step[1]
                    c = slice(p * 2 * P, (p + 1) * 2 * P)
                    reach(dve, ft_hi_ready, a, p + 1)
                    low(ft_lo[:, :, c], att_bank(("ft", p))[:, :].rearrange("p (k n) -> p k n", k=KT), ft_hi[:, :, c])\
                        .then_inc(ft_ready[0], 1)

            def hidden(e, m, f):
                reach(dve, silu_ready, f, 2 * e + m + 1)
                nc.vector.tensor_tensor(h_f[:, m, :], h_f[:, m, :], up_ps[m][:, :], ALU.mult).then_inc(h_ready[0], 1)

            def low_hidden(e, m, f):
                reach(dve, h_hi_ready, f, 2 * e + m + 1)
                low(h_lo[:, e % 2, m, :], h_f[:, m, :], h_hi[:, e % 2, m, :]).then_inc(h_lo_ready[0], 1)

            def add_down(e, p, f):
                if e == 0:
                    reach(dve, route_ready, f, 1)
                reach(dve, down_done, f, 2 * e + p + 1)
                for n in range(2):
                    t, src = 2 * p + n, down_ps[p][:, n * HID:(n + 1) * HID]
                    if e == 0:
                        last = nc.vector.tensor_scalar(acc[:, t, :], src, route[:, t, e:e + 1], None, ALU.mult)
                    else:
                        last = nc.vector.scalar_tensor_tensor(acc[:, t, :], src, route[:, t, e:e + 1], acc[:, t, :],
                                                              ALU.mult, ALU.add)
                last.then_inc(down_read[0], 1)

            def out_stats(f):
                reach(dve, down_read, f, 2 * E)
                ln_stats(4, acc, range(TILES), bn4, mv4, var4)

            def out_apply(f):
                reach(dve, rstd_ready[3], f, 1)
                settle(ln_apply(acc, acc, range(TILES), mv4, rstd4))
                reach(dve, x1_copied, f, 1)
                nc.vector.tensor_tensor(x1_kept[:, :, :], x1_kept[:, :, :], acc[:, :, :], ALU.add).then_inc(out_ready[0], 1)

            def route_rank(a):
                shape = [P, TILES, E, E]
                mine, other = (dist[:, :, :].unsqueeze(n).broadcast_to(shape) for n in (3, 2))
                reach(dve, dist_ready, a, 1)
                nc.vector.tensor_tensor(nearer[:, :, :, :], other, mine, ALU.is_lt)
                settle(nc.vector.tensor_tensor(as_near[:, :, :, :], other, mine, ALU.is_equal))
                settle(nc.vector.tensor_tensor(as_near[:, :, :, :], as_near[:, :, :, :],
                                               before[:, :, :, :].broadcast_to(shape), ALU.mult))
                settle(nc.vector.tensor_tensor(nearer[:, :, :, :], nearer[:, :, :, :], as_near[:, :, :, :], ALU.add))
                nc.vector.tensor_reduce(rank[:, :, :], nearer[:, :, :, :], AX.X, ALU.add).then_inc(rank_ready[0], 1)

            def route_weights(a):
                per_expert = [P, 2, TILES, E]
                reach(dve, rank_ready, a, 1)
                reach(dve, fallback_ready, a, 1)
                settle(nc.vector.tensor_tensor(cube[:, :, :], fallback[:, :, :], fallback[:, :, :], ALU.mult))
                nc.vector.scalar_tensor_tensor(kinds[:, 1, :, :], rank[:, :, :], 2.0, fallback[:, :, :], ALU.is_lt, ALU.mult)
                settle(nc.vector.tensor_tensor(cube[:, :, :], cube[:, :, :], fallback[:, :, :], ALU.mult))
                settle(nc.vector.tensor_tensor(kinds[:, 0, :, :], cube[:, :, :], zone[:, :, :], ALU.mult))
                settle(nc.vector.tensor_reduce(sums[:, :, :], kinds[:, :, :, :], AX.X, ALU.add))
                nc.vector.tensor_scalar(chosen[:, 0, :], sums[:, 0, :], TINY, None, ALU.is_ge)
                nc.vector.tensor_scalar(chosen[:, 1, :], sums[:, 0, :], TINY, None, ALU.is_lt)
                settle(nc.vector.tensor_scalar(guarded[:, :, :], sums[:, :, :], TINY, None, ALU.max))
                settle(nc.vector.reciprocal(guarded[:, :, :], guarded[:, :, :]))
                settle(nc.vector.tensor_tensor(guarded[:, :, :], guarded[:, :, :], chosen[:, :, :], ALU.mult))
                settle(nc.vector.tensor_tensor(kinds[:, :, :, :], kinds[:, :, :, :],
                                               guarded[:, :, :].unsqueeze(3).broadcast_to(per_expert), ALU.mult))
                nc.vector.tensor_tensor(route[:, :, :], kinds[:, 0, :, :], kinds[:, 1, :, :], ALU.add)\
                    .then_inc(route_ready[0], 1)

            def attention(n, a):
                for step in STEPS[n]:
                    att_step(step, a)

            def low_of_unit(u):
                dve.wait_ge(w_hi_ready, ATT_W + u + 1)
                low(w_lo[:, u, :, :], stage(u)[1], w_hi[:, u, :, :]).then_inc(w_ready, 1)

            dve.sem_inc(down_read[0], down_read[2])
            for j in range(HPG):
                nc.vector.memset(kz[:, :, j, :], 0.0)
            nc.vector.memset(state[:, :, :, :], 0.0)
            settle(nc.vector.memset(v_sb[:, :, :, D:VA], 1.0))
            dve.wait_ge(small_loaded, 48)
            dve.wait_ge(att_w_loaded[2], 16)
            for g in range(HG):
                last = nc.vector.tensor_scalar(wo_raw[:, g, :], wo_raw[:, g, :], nw[:, g:g + 1], None, ALU.mult)
            last.then_inc(wo_scaled, 1)
            dve.wait_ge(w_hi_ready, 1)
            low(wq_lo[:, :, :], wq_raw, wq_hi[:, :, :]).then_inc(w_ready, 1)
            dve.wait_ge(w_hi_ready, 2)
            low(wkv_lo[:, :, :], wkv_raw, wkv_hi[:, :, :]).then_inc(w_ready, 1)
            dve.wait_ge(w_hi_ready, 3)
            low(wo_lo[:, :, :], wo_raw, wo_hi[:, :, :]).then_inc(w_ready, 1)
            dve.wait_ge(wr_hi_ready, 1)
            low(wr_hl[:, :, E:2 * E], wr_raw[:, :, :], wr_hl[:, :, 0:E]).then_inc(wr_ready, 1)
            settle(nc.vector.reciprocal(half_inv_t[:, :], temp[:, :]))
            nc.vector.tensor_scalar(half_inv_t[:, :], half_inv_t[:, :], 0.5, None, ALU.mult).then_inc(temp_ready, 1)
            dve.wait_ge(const_ready, 1)
            for n in range(len(STEPS)):
                attention(n, (0, 0))
                if n < UNITS:
                    low_of_unit(n)
            route_rank((0, 0))
            hidden(0, 0, (0, 0))
            low_hidden(0, 0, (0, 0))
            hidden(0, 1, (0, 0))
            low_hidden(0, 1, (0, 0))
            route_weights((0, 0))
            with dve.Fori(1, BLOCKS) as i:
                a, f = (i, 0), (i, -1)
                for e in range(1, E - 1):
                    for m in range(MT):
                        hidden(e, m, f)
                        attention(4 * e - 4 + 2 * m, a)
                        low_hidden(e, m, f)
                        add_down(e - 1, m, f)
                        attention(4 * e - 3 + 2 * m, a)
                for m in range(MT):
                    hidden(E - 1, m, f)
                    attention(4 * E - 8 + 2 * m, a)
                    low_hidden(E - 1, m, f)
                    attention(4 * E - 7 + 2 * m, a)
                add_down(E - 2, 0, f)
                add_down(E - 2, 1, f)
                route_rank(a)
                for m in range(MT):
                    hidden(0, m, a)
                    low_hidden(0, m, a)
                    add_down(E - 1, m, f)
                out_stats(f)
                route_weights(a)
                out_apply(f)
            f = (BLOCKS - 1, 0)
            for e in range(1, E):
                for m in range(MT):
                    hidden(e, m, f)
                    low_hidden(e, m, f)
                    add_down(e - 1, m, f)
            add_down(E - 1, 0, f)
            add_down(E - 1, 1, f)
            out_stats(f)
            out_apply(f)

        @block_scope.gpsimd
        def _(pool):
            def settle(ins):
                ins.then_inc(pool_own, 1)
                pool.wait_ge(pool_own, 1).then_inc(pool_own, -1)

            def inverse_root(n, k, cols, a, var, rstd):
                reach(pool, var_ready[n - 1], a, k)
                nc.gpsimd.tensor_tensor(rstd[:, cols], var[:, cols], minus_half[:, 0:cols.stop - cols.start], ALU.pow)\
                    .then_inc(rstd_ready[n - 1][0], 1)

            def att_step(step, a):
                kind = step[0]
                if kind == "ln1_stats":
                    inverse_root(1, 1, slice(0, TILES), a, var1, rstd1)
                elif kind == "ln2_stats":
                    p = step[1]
                    inverse_root(2, p + 1, slice(2 * p, 2 * p + 2), a, var2, rstd2)
                elif kind == "ln3_stats":
                    p = step[1]
                    inverse_root(3, p + 1, slice(2 * p, 2 * p + 2), a, var3, rstd3)
                elif kind == "norm_stats":
                    t = step[1]
                    reach(pool, rms_in_ready, a, t + 1)
                    reach(pool, on_ready, a, t - 1)
                    nc.gpsimd.tensor_tensor(rms_f[:, t % 2, :], rms_in[:, :], minus_half[:, :], ALU.pow)\
                        .then_inc(rms_ready[0], 1)

            def routing(a):
                reach(pool, rz_copied, a, 1)
                nc.gpsimd.tensor_tensor(logit[:, :, :], rz[:, :, 0, :], rz[:, :, 1, :], ALU.add).then_inc(logit_ready[0], 1)
                reach(pool, tanh_ready, a, 1)
                settle(nc.gpsimd.tensor_tensor(inh[:, :, :], tanh[:, :, :],
                                               minus_one[:, :].unsqueeze(2).broadcast_to([P, TILES, E]), ALU.subtract))
                settle(nc.gpsimd.tensor_scalar(inh[:, :, :], inh[:, :, :], 0.5, None, ALU.mult))
                settle(nc.gpsimd.tensor_scalar(off[:, :, :], inh[:, :, :], CENTER, None, ALU.subtract))
                nc.gpsimd.tensor_scalar(neg_off[:, :, :], off[:, :, :], -1.0, 0.0, ALU.mult, ALU.max)
                settle(nc.gpsimd.tensor_scalar(off[:, :, :], off[:, :, :], 0.0, None, ALU.max))
                reach(pool, route_ready, a, 0)
                nc.gpsimd.tensor_tensor(dist[:, :, :], off[:, :, :], neg_off[:, :, :], ALU.add).then_inc(dist_ready[0], 1)
                nc.gpsimd.tensor_scalar(zone2[:, :, :], inh[:, :, :], UPPER, None, ALU.is_le)
                settle(nc.gpsimd.tensor_scalar(zone[:, :, :], inh[:, :, :], LOWER, None, ALU.is_ge))
                nc.gpsimd.tensor_tensor(zone[:, :, :], zone[:, :, :], zone2[:, :, :], ALU.mult)
                settle(nc.gpsimd.tensor_scalar(expo[:, :, :], dist[:, :, :], -1.0 / 0.3, None, ALU.mult))
                nc.gpsimd.tensor_tensor(fallback[:, :, :], euler[:, :, :], expo[:, :, :], ALU.pow)\
                    .then_inc(fallback_ready[0], 1)

            def attention(n, a):
                for step in STEPS[n]:
                    att_step(step, a)

            nc.gpsimd.memset(ident[:, :], 0.0)
            nc.gpsimd.memset(causal[:, :, :], 1.0)
            nc.gpsimd.memset(diag[:, :, :, :], 1.0)
            nc.gpsimd.memset(before[:, :, :, :], 1.0)
            nc.gpsimd.memset(minus_half[:, :], -0.5)
            nc.gpsimd.memset(minus_one[:, :], -1.0)
            settle(nc.gpsimd.memset(euler[:, :, :], math.e))
            nc.gpsimd.affine_select(out=ident[:, :], in_=ident[:, :], compare_op=ALU.not_equal, fill=1.0,
                                    base=0, pattern=[[-1, P]], channel_multiplier=1)
            nc.gpsimd.affine_select(out=causal[:, 0, :], in_=causal[:, 0, :], compare_op=ALU.is_ge, fill=0.0,
                                    base=0, pattern=[[1, P]], channel_multiplier=-1)
            nc.gpsimd.affine_select(out=before[:, 0, :, :], in_=before[:, 0, :, :], compare_op=ALU.is_ge, fill=0.0,
                                    base=-1, pattern=[[1, E], [-1, E]], channel_multiplier=0)
            settle(nc.gpsimd.affine_select(out=diag[:, 0, :, :], in_=diag[:, 0, :, :], compare_op=ALU.is_ge, fill=0.0,
                                           base=0, pattern=[[-D, HPG], [0, VA]], channel_multiplier=1))
            nc.gpsimd.affine_select(out=diag[:, 0, :, :], in_=diag[:, 0, :, :], compare_op=ALU.is_ge, fill=0.0,
                                    base=D - 1, pattern=[[D, HPG], [0, VA]], channel_multiplier=-1)\
                .then_inc(const_ready, 1)
            for n in range(len(STEPS)):
                attention(n, (0, 0))
            routing((0, 0))
            with pool.Fori(1, BLOCKS) as i:
                a, f = (i, 0), (i, -1)
                for n in range(len(STEPS)):
                    attention(n, a)
                routing(a)
                inverse_root(4, 1, slice(0, TILES), f, var4, rstd4)
            inverse_root(4, 1, slice(0, TILES), (BLOCKS - 1, 0), var4, rstd4)


def kernel(L0_attn_hidden_states, L0_attn_Wq, L0_attn_Wk, L0_attn_Wv, L0_attn_Wo, L0_attn_norm_w,
           L0_ffn_Wg, L0_ffn_Wu, L0_ffn_Wd, L0_ffn_Wr, L0_ffn_temperature):
    import numpy as np
    import concourse.bacc as bacc
    from concourse import mybir as _mybir
    from concourse.bass_utils import run_bass_kernel_spmd

    layouts = {
        "x": L0_attn_hidden_states,
        "wq_t": np.transpose(L0_attn_Wq),
        "wkv_t": np.concatenate([np.transpose(L0_attn_Wk), np.transpose(L0_attn_Wv)], axis=1),
        "wo_t": np.transpose(L0_attn_Wo),
        "norm_w": np.tile(L0_attn_norm_w, H).reshape(HG, P).T,
        "wg": L0_ffn_Wg,
        "wu": L0_ffn_Wu,
        "wd": L0_ffn_Wd,
        "wr": L0_ffn_Wr,
        "temperature": L0_ffn_temperature,
    }
    nc = bacc.Bacc("TRN2", target_bir_lowering=False, num_devices=1)
    arrays, args = {}, []
    for name, a in layouts.items():
        a = np.ascontiguousarray(a)
        arrays[f"in_{name}"] = a
        args.append(nc.dram_tensor(f"in_{name}", a.shape, _mybir.dt.from_np(a.dtype), kind="ExternalInput").ap())
    args.append(nc.dram_tensor("out_rows", (B, S, HID), _mybir.dt.float32, kind="ExternalOutput").ap())
    build_program(nc, *args)
    result = run_bass_kernel_spmd(nc, [arrays], core_ids=[0])
    return result.results[0]["out_rows"]
```

```python
import math
from contextlib import ExitStack

import concourse.bass as bass
from concourse import mybir

B, S, HID = 2, 4096, 256
H, D = 8, 32
E, INNER = 8, 256
P = 128
KT = HID // P
HG = H * D // P
HPG = H // HG
MT = INNER // P
CHUNK = P
ROWS = 256
BLOCKS = S // ROWS
TILES = B * ROWS // P
TOK = TILES * P
VA = D + 1
GV = HPG * VA

LN_EPS = 1e-5
RMS_EPS = 1e-5
DENOM_EPS = 1.0
CENTER = 1.0 / math.e
LOWER = 0.5 - math.log(4.0 / 3.0)
UPPER = 0.5
TINY = 1e-8

STEPS = [
    [("xt", 0), ("xt", 1)],
    [("kv", 0), ("q", 0)],
    [("q", 1), ("kt", 0)],
    [("kv", 1)],
    [("s", 0, 0)],
    [("s", 0, 1), ("kt", 1)],
    [("o", 0), ("su", 0)],
    [("s", 1, 0), ("kv", 2), ("keep_x1",)],
    [("s", 1, 1), ("norm_stats", 0)],
    [("o", 1), ("su", 1), ("kt", 2), ("norm_apply", 0)],
    [("s", 2, 0), ("ot", 0)],
    [("s", 2, 1), ("norm_stats", 1), ("kv", 3)],
    [("o", 2), ("su", 2), ("kt", 3), ("norm_apply", 1)],
    [("s", 3, 0), ("ot", 1)],
    [("s", 3, 1), ("norm_stats", 2), ("wo", 0)],
    [("o", 3), ("su", 3), ("norm_apply", 2), ("ln2_stats", 0)],
    [("norm_stats", 3), ("ot", 2), ("ln2_apply", 0)],
    [("norm_apply", 3), ("ln2_add", 0), ("ln3_stats", 0)],
    [("ot", 3), ("ln3_apply", 0)],
    [("wo", 1)],
    [("ln2_stats", 1)],
    [("ln2_apply", 1)],
    [("ft", 0), ("ln2_add", 1), ("ln3_stats", 1)],
    [],
    [("ln3_apply", 1)],
    [("ft", 1)],
    [("ft_out", 0)],
    [("ft_out", 1)],
]
ROUTER = ("r",)
PSUM_STEPS = [s for after in STEPS for s in after if s[0] in ("xt", "q", "kv", "kt", "s", "o", "su", "ot", "wo", "ft")]
PSUM_STEPS.append(ROUTER)
NUMBER = {s: n for n, s in enumerate(PSUM_STEPS)}
N_PSUM = len(PSUM_STEPS)


def build_program(nc, x, wq_t, wkv_t, wo_t, norm_w, wg, wu, wd, wr, temperature, out):
    f32, f32r = mybir.dt.float32, mybir.dt.float32r
    ALU, ACT, AX = mybir.AluOpType, mybir.ActivationFunctionType, mybir.AxisListType

    ctx = ExitStack()
    with ctx:
        def sb(name, shape, dt=f32):
            return ctx.enter_context(nc.sbuf_tensor(name, shape, dt))

        def sem(name):
            return ctx.enter_context(nc.semaphore(name))

        w_hi = sb("w_hi", [P, 3 * E, 2, 256], f32r)
        w_lo = sb("w_lo", [P, 3 * E, 2, 256], f32r)
        wq_hi, wq_lo = sb("wq_hi", [P, KT, HID], f32r), sb("wq_lo", [P, KT, HID], f32r)
        wkv_hi, wkv_lo = sb("wkv_hi", [P, KT, 2 * HID], f32r), sb("wkv_lo", [P, KT, 2 * HID], f32r)
        wo_hi, wo_lo = sb("wo_hi", [P, HG, HID], f32r), sb("wo_lo", [P, HG, HID], f32r)
        wr_raw = sb("wr_raw", [P, KT, E])
        wr_hl = sb("wr_hl", [P, KT, 2 * E], f32r)
        wr_h0 = sb("wr_h0", [P, KT, 2 * E], f32r)
        nw = sb("nw", [P, HG])
        temp = sb("temp", [P, 1])
        half_inv_t = sb("half_inv_t", [P, 1])

        xs = sb("xs", [P, TILES, HID])
        rows = sb("rows", [P, TILES, HID])
        xt_hi, xt_lo = sb("xt_hi", [P, KT, TOK], f32r), sb("xt_lo", [P, KT, TOK], f32r)
        q_t = sb("q_t", [P, HG, TOK])
        k_sb = sb("k_sb", [P, TILES, H * D])
        v_sb = sb("v_sb", [P, TILES, H, VA])
        kz = sb("kz", [P, HG, HPG, P])
        prob = sb("prob", [P, H, P])
        fin = prob[:, :, :].rearrange("p (t a) n -> p t (a n)", t=TILES)
        state = sb("state", [P, B, HG, GV])
        state_add = sb("state_add", [P, HG, GV])
        o_sb = sb("o_sb", [P, 2, H, VA])
        o_sq = sb("o_sq", [P, H, VA])
        o_n = sb("o_n", [P, 2, H, D])
        ot_hi, ot_lo = (xt[:, 0, :].rearrange("p (a g n) -> p a g n", a=2, g=HG) for xt in (xt_hi, xt_lo))
        x1 = sb("x1", [P, TILES, HID])

        ft_hi, ft_lo = sb("ft_hi", [P, KT, TOK], f32r), sb("ft_lo", [P, KT, TOK], f32r)
        h_hi, h_lo = sb("h_hi", [P, 2, MT, TOK], f32r), sb("h_lo", [P, 2, MT, TOK], f32r)
        NSTAGE = 6
        late = sb("late", [P, NSTAGE * 512])
        h_f = late[:, 0:1024].rearrange("p (m n) -> p m n", m=MT)
        acc = late[:, 1024:2048].rearrange("p (t n) -> p t n", t=TILES)
        x1_kept = late[:, 2048:3072].rearrange("p (t n) -> p t n", t=TILES)

        bn1, bn2, bn3, bn4 = (sb(f"bn{n}", [P, TILES, 6]) for n in (1, 2, 3, 4))
        mv1, mv2, mv3, mv4 = (sb(f"mv{n}", [P, TILES, 2]) for n in (1, 2, 3, 4))
        var1, var2, var3, var4 = (sb(f"var{n}", [P, TILES]) for n in (1, 2, 3, 4))
        rstd1, rstd2, rstd3, rstd4 = (sb(f"rstd{n}", [P, TILES]) for n in (1, 2, 3, 4))
        shift1, shift2, shift3, shift4 = (sb(f"shift{n}", [P, TILES]) for n in (1, 2, 3, 4))
        den2, ssq = sb("den2", [P, H]), sb("ssq", [P, H])
        rms_in, rms_f = sb("rms_in", [P, H]), sb("rms_f", [P, 2, H])
        ident = sb("ident", [P, P])
        causal = sb("causal", [P, 1, P])
        diag = sb("diag", [P, 1, HPG, VA])
        before = sb("before", [P, 1, E, E])
        minus_half, minus_one = sb("minus_half", [P, H]), sb("minus_one", [P, TILES])
        euler = sb("euler", [P, TILES, E])
        rz = sb("rz", [P, TILES, 2, E])
        logit, tanh, inh = (sb(n, [P, TILES, E]) for n in ("logit", "tanh", "inh"))
        off, neg_off, dist, zone, zone2 = (sb(n, [P, TILES, E]) for n in ("off", "neg_off", "dist", "zone", "zone2"))
        expo, fallback, cube, rank = (sb(n, [P, TILES, E]) for n in ("expo", "fallback", "cube", "rank"))
        nearer, as_near = sb("nearer", [P, TILES, E, E]), sb("as_near", [P, TILES, E, E])
        kinds = sb("kinds", [P, 2, TILES, E])
        sums, guarded, chosen = (sb(n, [P, 2, TILES]) for n in ("sums", "guarded", "chosen"))
        route = sb("route", [P, TILES, E])

        def bank(name):
            return ctx.enter_context(nc.psum_tensor(name, [P, 512], f32))

        gate_ps = [bank(f"gate_ps{m}") for m in range(MT)]
        up_ps = [bank(f"up_ps{m}") for m in range(MT)]
        down_ps = [bank(f"down_ps{p}") for p in range(2)]
        att_ps = [bank(f"att_ps{n}") for n in range(2)]

        def counter(name, per_block, before_first=0):
            return sem(name), per_block, before_first

        x_loaded = counter("x_loaded", 32)
        out_stored = counter("out_stored", 32, 32)
        att_done = counter("att_done", N_PSUM)
        xn_ready = counter("xn_ready", 1)
        xt_hi_ready = counter("xt_hi_ready", KT)
        xt_ready = counter("xt_ready", KT)
        q_ready = counter("q_ready", HG)
        k_ready = counter("k_ready", TILES)
        v_ready = counter("v_ready", TILES)
        kz_ready = counter("kz_ready", TILES)
        prob_ready = counter("prob_ready", TILES * HG)
        o_copied = counter("o_copied", TILES)
        o_squared = counter("o_squared", TILES)
        rms_in_ready = counter("rms_in_ready", TILES)
        rms_ready = counter("rms_ready", TILES)
        on_ready = counter("on_ready", TILES)
        su_read = counter("su_read", TILES)
        state_ready = counter("state_ready", TILES)
        ot_hi_ready = counter("ot_hi_ready", TILES)
        ot_ready = counter("ot_ready", TILES)
        wo_copied = counter("wo_copied", 2)
        x1_ready = counter("x1_ready", 2)
        ln2_applied = counter("ln2_applied", 2)
        x1n_ready = counter("x1n_ready", 2)
        fin_ready = counter("fin_ready", 1)
        x1_copied = counter("x1_copied", 1)
        ft_hi_ready = counter("ft_hi_ready", 2)
        ft_ready = counter("ft_ready", 2)
        moments_ready = [counter(f"moments{n}_ready", k) for n, k in ((1, 1), (2, 2), (3, 2), (4, 1))]
        rstd_ready = [counter(f"rstd{n}_ready", k) for n, k in ((1, 1), (2, 2), (3, 2), (4, 1))]
        rz_copied = counter("rz_copied", 1)
        logit_ready = counter("logit_ready", 1)
        tanh_ready = counter("tanh_ready", 1)
        dist_ready = counter("dist_ready", 1)
        fallback_ready = counter("fallback_ready", 1)
        rank_ready = counter("rank_ready", 1)
        route_ready = counter("route_ready", 1)
        up_done = counter("up_done", 2 * E)
        silu_ready = counter("silu_ready", 2 * E)
        h_ready = counter("h_ready", 2 * E)
        h_hi_ready = counter("h_hi_ready", 2 * E)
        h_lo_ready = counter("h_lo_ready", 2 * E)
        down_done = counter("down_done", 2 * E)
        down_read = counter("down_read", 2 * E)
        out_ready = counter("out_ready", 1)
        att_w_loaded = [sem(f"att_w_loaded{n}") for n in range(3)]
        small_loaded = sem("small_loaded")
        stage_loaded = [sem(f"stage_loaded{n}") for n in range(NSTAGE)]
        w_hi_ready = sem("w_hi_ready")
        w_ready = sem("w_ready")
        wo_scaled = sem("wo_scaled")
        wr_hi_ready = sem("wr_hi_ready")
        wr_ready = sem("wr_ready")
        temp_ready = sem("temp_ready")
        const_ready = sem("const_ready")
        dve_own, pool_own = sem("dve_own"), sem("pool_own")

        def reach(eng, count, block, k):
            s, per_block, first = count
            base, offset = block
            value = offset * per_block + k + first
            if isinstance(base, int):
                if base * per_block + value > first:
                    eng.wait_ge(s, base * per_block + value)
            else:
                eng.wait_ge(s, base * per_block + value)

        READ_OUT = {ROUTER: (rz_copied, 1)}
        for n in range(KT):
            READ_OUT["xt", n] = (xt_ready, n + 1)
        for n in range(HG):
            READ_OUT["q", n] = (q_ready, n + 1)
        for t in range(TILES):
            READ_OUT["kv", t] = (v_ready, t + 1)
            READ_OUT["kt", t] = (kz_ready, t + 1)
            for g in range(HG):
                READ_OUT["s", t, g] = (prob_ready, HG * t + g + 1)
            READ_OUT["o", t] = (o_copied, t + 1)
            READ_OUT["su", t] = (su_read, t + 1)
            READ_OUT["ot", t] = (ot_ready, t + 1)
        for p in range(2):
            READ_OUT["wo", p] = (wo_copied, p + 1)
            READ_OUT["ft", p] = (ft_ready, p + 1)

        def att_bank(step):
            return att_ps[NUMBER[step] % 2]

        UNITS = 3 * E

        def unit_src(u):
            return (wg, wu, wd)[u % 3][u // 3, :, :].rearrange("(k p) n -> p k n", p=P)

        def stage(u):
            n = (u + 4) % NSTAGE
            return n, late[:, 512 * n:512 * n + 512].rearrange("p (k n) -> p k n", k=2)

        wq_raw = late[:, 0:512].rearrange("p (k n) -> p k n", k=KT)
        wkv_raw = late[:, 512:1536].rearrange("p (k n) -> p k n", k=KT)
        wo_raw = late[:, 1536:2048].rearrange("p (k n) -> p k n", k=HG)
        ATT_W = 3

        def rows_of(dram, b, row):
            return dram[b, bass.ds(row, ROWS), :].rearrange("(c p) n -> p c n", p=P)

        def tiles_of(tensor, b):
            return tensor[:, b:TILES:B, :]

        block_scope = ctx.enter_context(nc.Block())

        @block_scope.sync
        def _(sp):
            def load_x(row):
                for b in range(B):
                    sp.dma_start(tiles_of(xs, b), rows_of(x, b, row)).then_inc(x_loaded[0], 16)

            def store_out(block, row):
                reach(sp, out_ready, block, 1)
                for b in range(B):
                    sp.dma_start(rows_of(out, b, row), tiles_of(x1_kept, b)).then_inc(out_stored[0], 16)

            sp.sem_inc(out_stored[0], out_stored[2])
            load_x(0)
            sp.dma_start(wq_raw, wq_t.rearrange("(k p) n -> p k n", p=P)).then_inc(att_w_loaded[0], 16)
            sp.dma_start(wkv_raw, wkv_t.rearrange("(k p) n -> p k n", p=P)).then_inc(att_w_loaded[1], 16)
            sp.dma_start(nw[:, :], norm_w).then_inc(small_loaded, 16)
            sp.dma_start(wr_raw[:, :, :], wr.rearrange("(k p) n -> p k n", p=P)).then_inc(small_loaded, 16)
            sp.dma_start(temp[:, :], temperature.partition_broadcast(P)).then_inc(small_loaded, 16)
            sp.dma_start(wo_raw, wo_t.rearrange("(k p) n -> p k n", p=P)).then_inc(att_w_loaded[2], 16)
            for u in range(UNITS):
                n, slot = stage(u)
                if u >= 2:
                    sp.wait_ge(w_ready, {2: 1, 3: 2, 4: 2, 5: 3}.get(u, ATT_W + u - NSTAGE + 1))
                sp.dma_start(slot, unit_src(u)).then_inc(stage_loaded[n], 16)
            reach(sp, x1_ready, (0, 0), 2)
            load_x(ROWS)
            with sp.Fori(1, BLOCKS - 1) as i:
                reach(sp, x1_ready, (i, 0), 2)
                load_x(i * ROWS + ROWS)
                store_out((i, -1), i * ROWS - ROWS)
            store_out((BLOCKS - 2, 0), (BLOCKS - 2) * ROWS)
            store_out((BLOCKS - 1, 0), (BLOCKS - 1) * ROWS)
            reach(sp, out_stored, (BLOCKS, 0), 0)

        @block_scope.tensor
        def _(pe):
            def products(dst, pairs, start=True, stop=True):
                terms = [t for (l_hi, l_lo), (r_hi, r_lo) in pairs
                         for t in ((l_hi, r_hi), (l_hi, r_lo), (l_lo, r_hi))]
                for n, (lhs, rhs) in enumerate(terms):
                    last = nc.tensor.matmul(dst, lhs, rhs, start=start and n == 0, stop=stop and n == len(terms) - 1)
                return last

            def att_step(step, a):
                if step not in NUMBER:
                    return
                kind, dst, number = step[0], att_bank(step), NUMBER[step]
                before_it = [m for m in range(number) if m % 2 == number % 2]
                if before_it:
                    reach(pe, READ_OUT[PSUM_STEPS[before_it[-1]]][0], a, READ_OUT[PSUM_STEPS[before_it[-1]]][1])
                else:
                    m = max(m for m in range(N_PSUM) if m % 2 == number % 2)
                    count, k = READ_OUT[PSUM_STEPS[m]]
                    reach(pe, count, (a[0], a[1] - 1), k)
                if kind == "xt":
                    k = step[1]
                    reach(pe, xn_ready, a, 1)
                    for t in range(TILES):
                        last = nc.tensor.transpose(dst[:, t * P:t * P + P], rows[:, t, k * P:k * P + P], ident[:, :])
                elif kind == "q":
                    g = step[1]
                    reach(pe, xt_ready, a, KT)
                    last = products(dst[:, :], [((wq_hi[:, k, g * P:g * P + P], wq_lo[:, k, g * P:g * P + P]),
                                                 (xt_hi[:, k, :], xt_lo[:, k, :])) for k in range(KT)])
                elif kind == "kv":
                    t = slice(step[1] * P, step[1] * P + P)
                    reach(pe, xt_ready, a, KT)
                    last = products(dst[:, :], [((xt_hi[:, k, t], xt_lo[:, k, t]), (wkv_hi[:, k, :], wkv_lo[:, k, :]))
                                                for k in range(KT)])
                elif kind == "kt":
                    t = step[1]
                    reach(pe, k_ready, a, t + 1)
                    for g in range(HG):
                        last = nc.tensor.transpose(dst[:, g * P:g * P + P], k_sb[:, t, g * P:g * P + P], ident[:, :])
                elif kind == "s":
                    t, g = step[1:]
                    reach(pe, q_ready, a, g + 1)
                    reach(pe, kz_ready, a, t + 1)
                    for j in range(HPG):
                        last = nc.tensor.matmul(dst[:, j * P:j * P + P], kz[:, g, j, :], q_t[:, g, t * P:t * P + P],
                                                start=True, stop=True)
                elif kind == "o":
                    t = step[1]
                    reach(pe, prob_ready, a, HG * t + HG)
                    reach(pe, v_ready, a, t + 1)
                    reach(pe, state_ready, a, t - B + 1)
                    for g in range(HG):
                        nc.tensor.matmul(dst[:, g * GV:g * GV + GV], q_t[:, g, t * P:t * P + P], state[:, t % B, g, :],
                                         start=True, stop=False)
                        for j in range(HPG):
                            h = g * HPG + j
                            last = nc.tensor.matmul(dst[:, h * VA:h * VA + VA], prob[:, h, :], v_sb[:, t, h, :],
                                                    start=False, stop=j == HPG - 1)
                elif kind == "su":
                    t = step[1]
                    for g in range(HG):
                        last = nc.tensor.matmul(dst[:, g * GV:g * GV + GV], k_sb[:, t, g * P:g * P + P],
                                                v_sb[:, t, g * HPG:g * HPG + HPG, :], start=True, stop=True)
                elif kind == "ot":
                    t = step[1]
                    reach(pe, on_ready, a, t + 1)
                    for g in range(HG):
                        last = nc.tensor.transpose(dst[:, g * P:g * P + P], o_n[:, t % 2, g * HPG:g * HPG + HPG, :],
                                                   ident[:, :])
                elif kind == "wo":
                    p = step[1]
                    reach(pe, ot_ready, a, 2 * p + 2)
                    for t in range(2):
                        last = products(dst[:, t * HID:t * HID + HID],
                                        [((ot_hi[:, t, g, :], ot_lo[:, t, g, :]), (wo_hi[:, g, :], wo_lo[:, g, :]))
                                         for g in range(HG)])
                elif kind == "ft":
                    p = step[1]
                    reach(pe, x1n_ready, a, p + 1)
                    for k in range(KT):
                        for t in range(2):
                            c = (2 * k + t) * P
                            last = nc.tensor.transpose(dst[:, c:c + P], rows[:, 2 * p + t, k * P:k * P + P], ident[:, :])
                elif kind == "r":
                    reach(pe, ft_ready, a, 2)
                    for t in range(TILES):
                        cols, ts = dst[:, t * 2 * E:(t + 1) * 2 * E], slice(t * P, t * P + P)
                        for k in range(KT):
                            nc.tensor.matmul(cols, ft_hi[:, k, ts], wr_hl[:, k, :], start=k == 0, stop=False)
                            last = nc.tensor.matmul(cols, ft_lo[:, k, ts], wr_h0[:, k, :], start=False, stop=k == KT - 1)
                last.then_inc(att_done[0], 1)

            def up(e, m, f):
                reach(pe, ft_ready, f, 2)
                reach(pe, h_ready, f, 2 * e + m - 1)
                c = slice(m * P, m * P + P)
                for n, dst in ((0, gate_ps[m]), (1, up_ps[m])):
                    last = products(dst[:, :], [((w_hi[:, 3 * e + n, k, c], w_lo[:, 3 * e + n, k, c]),
                                                 (ft_hi[:, k, :], ft_lo[:, k, :])) for k in range(KT)])
                last.then_inc(up_done[0], 1)

            def down(e, p, f):
                reach(pe, h_lo_ready, f, 2 * e + 2)
                reach(pe, down_read, f, 2 * e + p - 1)
                for t in range(2):
                    c = slice((2 * p + t) * P, (2 * p + t) * P + P)
                    last = products(down_ps[p][:, t * HID:t * HID + HID],
                                    [((h_hi[:, e % 2, m, c], h_lo[:, e % 2, m, c]),
                                      (w_hi[:, 3 * e + 2, m, :], w_lo[:, 3 * e + 2, m, :])) for m in range(MT)])
                last.then_inc(down_done[0], 1)

            def attention(n, a):
                for step in STEPS[n]:
                    att_step(step, a)

            def first_expert(a, f):
                attention(0, a)
                for m in range(MT):
                    up(1, m, f)
                    if m > 0:
                        attention(2 * m, a)
                    down(0, m, f)
                    attention(2 * m + 1, a)

            def rest(a, f):
                for e in range(2, E - 1):
                    for m in range(MT):
                        up(e, m, f)
                        attention(4 * e - 4 + 2 * m, a)
                        down(e - 1, m, f)
                        attention(4 * e - 3 + 2 * m, a)
                up(E - 1, 0, f)
                up(E - 1, 1, f)
                down(E - 2, 0, f)
                for n in range(4 * E - 8, 4 * E - 4):
                    attention(n, a)
                down(E - 2, 1, f)
                att_step(ROUTER, a)
                for m in range(MT):
                    up(0, m, a)
                    down(E - 1, m, f)

            pe.wait_ge(const_ready, 1)
            pe.wait_ge(w_ready, ATT_W)
            for n in range(len(STEPS)):
                attention(n, (0, 0))
            pe.wait_ge(wr_ready, 1)
            att_step(ROUTER, (0, 0))
            pe.wait_ge(w_ready, ATT_W + UNITS)
            up(0, 0, (0, 0))
            up(0, 1, (0, 0))
            first_expert((1, 0), (0, 0))
            with pe.Fori(1, BLOCKS - 1) as i:
                rest((i, 0), (i, -1))
                first_expert((i, 1), (i, 0))
            rest((BLOCKS - 1, 0), (BLOCKS - 2, 0))
            f = (BLOCKS - 1, 0)
            for e in range(1, E):
                for m in range(MT):
                    up(e, m, f)
                    down(e - 1, m, f)
            down(E - 1, 0, f)
            down(E - 1, 1, f)

        @block_scope.scalar
        def _(act):
            def copy(dst, src):
                return nc.scalar.activation(dst, src, ACT.Copy)

            def ln_apply(n, k, a, dst, src, tiles, shift, rstd):
                reach(act, rstd_ready[n - 1], a, k)
                for t in tiles:
                    last = nc.scalar.activation(dst[:, t, :], src[:, t, :], ACT.Identity, bias=shift[:, t:t + 1],
                                                scale=rstd[:, t:t + 1])
                return last

            def normalise_x(a):
                ln_apply(1, 1, a, rows, xs, range(TILES), shift1, rstd1).then_inc(xn_ready[0], 1)

            def normalise_out(f):
                ln_apply(4, 1, f, fin, fin, range(TILES), shift4, rstd4).then_inc(fin_ready[0], 1)

            def att_step(step, a):
                kind = step[0]
                if step in NUMBER and kind not in ("s", "su", "ft"):
                    reach(act, att_done, a, NUMBER[step] + 1)
                    src = att_bank(step)
                if kind == "xt":
                    copy(xt_hi[:, step[1], :], src[:, :]).then_inc(xt_hi_ready[0], 1)
                elif kind == "q":
                    copy(q_t[:, step[1], :], src[:, :]).then_inc(q_ready[0], 1)
                elif kind == "kv":
                    t = step[1]
                    copy(k_sb[:, t, :], src[:, 0:HID]).then_inc(k_ready[0], 1)
                    copy(v_sb[:, t, :, 0:D], src[:, HID:2 * HID].rearrange("p (h d) -> p h d", h=H))\
                        .then_inc(v_ready[0], 1)
                elif kind == "kt":
                    for j in range(HPG):
                        r = slice(j * D, j * D + D)
                        last = copy(kz[r, :, j, :], src[r, 0:HG * P].rearrange("p (g s) -> p g s", g=HG))
                    last.then_inc(kz_ready[0], 1)
                elif kind == "o":
                    t = step[1]
                    reach(act, on_ready, a, t - 1)
                    copy(o_sb[:, t % 2, :, :], src[:, 0:H * VA].rearrange("p (h v) -> p h v", h=H))\
                        .then_inc(o_copied[0], 1)
                    reach(act, rms_in_ready, a, t)
                    reach(act, o_copied, a, t + 1)
                    nc.scalar.activation(o_sq[:, :, :], o_sb[:, t % 2, :, :], ACT.Square).then_inc(o_squared[0], 1)
                elif kind == "ot":
                    t = step[1]
                    copy(ot_hi[:, t % 2, :, :], src[:, 0:HG * P].rearrange("p (g n) -> p g n", g=HG))\
                        .then_inc(ot_hi_ready[0], 1)
                elif kind == "wo":
                    p = step[1]
                    copy(rows[:, 2 * p:2 * p + 2, :], src[:, :].rearrange("p (t n) -> p t n", t=2))\
                        .then_inc(wo_copied[0], 1)
                elif kind == "ft_out":
                    p = step[1]
                    reach(act, att_done, a, NUMBER["ft", p] + 1)
                    reach(act, up_done, a, 0)
                    copy(ft_hi[:, :, p * 2 * P:(p + 1) * 2 * P], att_bank(("ft", p))[:, :].rearrange("p (k n) -> p k n", k=KT))\
                        .then_inc(ft_hi_ready[0], 1)
                elif kind == "ln2_apply":
                    p = step[1]
                    ln_apply(2, p + 1, a, rows, rows, range(2 * p, 2 * p + 2), shift2, rstd2).then_inc(ln2_applied[0], 1)
                elif kind == "ln3_apply":
                    p = step[1]
                    ln_apply(3, p + 1, a, rows, x1, range(2 * p, 2 * p + 2), shift3, rstd3).then_inc(x1n_ready[0], 1)
                elif kind == "r":
                    reach(act, logit_ready, a, 0)
                    copy(rz[:, :, :, :], src[:, 0:TILES * 2 * E].rearrange("p (t a e) -> p t a e", t=TILES, a=2))\
                        .then_inc(rz_copied[0], 1)

            def router_tanh(a):
                reach(act, logit_ready, a, 1)
                reach(act, dist_ready, a, 0)
                nc.scalar.activation(tanh[:, :, :], logit[:, :, :], ACT.Tanh, scale=half_inv_t[:, 0:1])\
                    .then_inc(tanh_ready[0], 1)

            def keep_x1(f):
                reach(act, x1_ready, f, 2)
                reach(act, out_stored, f, 0)
                copy(x1_kept[:, :, :], x1[:, :, :]).then_inc(x1_copied[0], 1)

            def silu(e, m, f):
                reach(act, up_done, f, 2 * e + m + 1)
                reach(act, h_lo_ready, f, 2 * e + m - 1)
                nc.scalar.activation(h_f[:, m, :], gate_ps[m][:, :], ACT.Silu).then_inc(silu_ready[0], 1)

            def high(e, m, f):
                reach(act, h_ready, f, 2 * e + m + 1)
                reach(act, down_done, f, 2 * e - 2)
                copy(h_hi[:, e % 2, m, :], h_f[:, m, :]).then_inc(h_hi_ready[0], 1)

            def attention(n, a, f=None):
                for step in STEPS[n]:
                    if step[0] == "keep_x1":
                        if f is not None:
                            keep_x1(f)
                    else:
                        att_step(step, a)

            def high_of_unit(u):
                n, raw = stage(u)
                act.wait_ge(stage_loaded[n], 16 * ((u // NSTAGE) + 1))
                copy(w_hi[:, u, :, :], raw).then_inc(w_hi_ready, 1)

            act.wait_ge(att_w_loaded[0], 16)
            copy(wq_hi[:, :, :], wq_raw).then_inc(w_hi_ready, 1)
            act.wait_ge(att_w_loaded[1], 16)
            copy(wkv_hi[:, :, :], wkv_raw).then_inc(w_hi_ready, 1)
            act.wait_ge(wo_scaled, 1)
            copy(wo_hi[:, :, :], wo_raw).then_inc(w_hi_ready, 1)
            act.wait_ge(small_loaded, 48)
            copy(wr_hl[:, :, 0:E], wr_raw[:, :, :])
            copy(wr_h0[:, :, 0:E], wr_raw[:, :, :])
            nc.scalar.activation(wr_h0[:, :, E:2 * E], wr_raw[:, :, :], ACT.Copy, scale=0.0).then_inc(wr_hi_ready, 1)
            def first_expert(a, f, done):
                if a is not None:
                    attention(0, a, f)
                silu(1, 0, f)
                high(1, 0, f)
                if a is not None:
                    attention(1, a, f)
                if done is not None:
                    normalise_out(done)
                silu(1, 1, f)
                if a is not None:
                    attention(2, a, f)
                high(1, 1, f)
                if a is not None:
                    attention(3, a, f)

            def rest(a, f, more=True):
                for e in range(2, E - 1):
                    for m in range(MT):
                        silu(e, m, f)
                        attention(4 * e - 4 + 2 * m, a, f)
                        high(e, m, f)
                        attention(4 * e - 3 + 2 * m, a, f)
                silu(E - 1, 0, f)
                high(E - 1, 0, f)
                attention(4 * E - 8, a, f)
                attention(4 * E - 7, a, f)
                silu(E - 1, 1, f)
                attention(4 * E - 6, a, f)
                high(E - 1, 1, f)
                attention(4 * E - 5, a, f)
                att_step(ROUTER, a)
                silu(0, 0, a)
                high(0, 0, a)
                router_tanh(a)
                if more:
                    normalise_x((a[0], a[1] + 1))
                silu(0, 1, a)
                high(0, 1, a)

            normalise_x((0, 0))
            for n in range(len(STEPS)):
                attention(n, (0, 0))
                if n < UNITS:
                    high_of_unit(n)
            act.wait_ge(temp_ready, 1)
            act.wait_ge(w_ready, ATT_W + UNITS)
            att_step(ROUTER, (0, 0))
            silu(0, 0, (0, 0))
            high(0, 0, (0, 0))
            router_tanh((0, 0))
            normalise_x((1, 0))
            silu(0, 1, (0, 0))
            high(0, 1, (0, 0))
            first_expert((1, 0), (0, 0), None)
            with act.Fori(1, BLOCKS - 1) as i:
                rest((i, 0), (i, -1))
                first_expert((i, 1), (i, 0), (i, -1))
            rest((BLOCKS - 1, 0), (BLOCKS - 2, 0), more=False)
            f = (BLOCKS - 1, 0)
            first_expert(None, f, (BLOCKS - 2, 0))
            keep_x1(f)
            for e in range(2, E):
                for m in range(MT):
                    silu(e, m, f)
                    high(e, m, f)
            normalise_out(f)

        @block_scope.vector
        def _(dve):
            def settle(ins):
                ins.then_inc(dve_own, 1)
                dve.wait_ge(dve_own, 1).then_inc(dve_own, -1)

            def low(dst, src, high_part):
                return nc.vector.tensor_tensor(dst, src, high_part.bitcast(f32), ALU.subtract)

            def ln_stats(n, src, tiles, bn, mv):
                for t in tiles:
                    last = nc.vector.bn_stats(bn[:, t, :], src[:, t, :])
                settle(last)
                for t in tiles:
                    last = nc.vector.bn_aggr(mv[:, t, :], bn[:, t, :])
                last.then_inc(moments_ready[n - 1][0], 1)

            def x_stats(a):
                reach(dve, x_loaded, a, 32)
                ln_stats(1, xs, range(TILES), bn1, mv1)

            def att_step(step, a):
                kind = step[0]
                if kind == "xt":
                    k = step[1]
                    reach(dve, xt_hi_ready, a, k + 1)
                    low(xt_lo[:, k, :], att_bank(step)[:, :], xt_hi[:, k, :]).then_inc(xt_ready[0], 1)
                elif kind == "s":
                    t, g = step[1:]
                    reach(dve, att_done, a, NUMBER[step] + 1)
                    nc.vector.tensor_tensor(prob[:, g * HPG:(g + 1) * HPG, :],
                                            att_bank(step)[:, :].rearrange("p (h n) -> p h n", h=HPG),
                                            causal[:, :, :].broadcast_to([P, HPG, P]), ALU.mult)\
                        .then_inc(prob_ready[0], 1)
                elif kind == "su":
                    t = step[1]
                    reach(dve, att_done, a, NUMBER[step] + 1)
                    nc.vector.tensor_tensor(state_add[:, :, :], att_bank(step)[:, 0:HG * GV].rearrange("p (g v) -> p g v", g=HG),
                                            diag[:, :, :, :].rearrange("p a j v -> p a (j v)").broadcast_to([P, HG, GV]),
                                            ALU.mult).then_inc(su_read[0], 1)
                    reach(dve, su_read, a, t + 1)
                    nc.vector.tensor_tensor(state[:, t % B, :, :], state[:, t % B, :, :], state_add[:, :, :], ALU.add)\
                        .then_inc(state_ready[0], 1)
                elif kind == "norm_stats":
                    t = step[1]
                    reach(dve, o_squared, a, t + 1)
                    nc.vector.tensor_scalar(den2[:, :], o_sq[:, :, D], DENOM_EPS ** 2, RMS_EPS, ALU.max, ALU.mult)
                    settle(nc.vector.tensor_reduce(ssq[:, :], o_sq[:, :, 0:D], AX.X, ALU.add))
                    nc.vector.scalar_tensor_tensor(rms_in[:, :], ssq[:, :], 1.0 / D, den2[:, :], ALU.mult, ALU.add)\
                        .then_inc(rms_in_ready[0], 1)
                elif kind == "norm_apply":
                    t = step[1]
                    reach(dve, rms_ready, a, t + 1)
                    if t >= 2:
                        reach(dve, att_done, a, NUMBER["ot", t - 2] + 1)
                    nc.vector.tensor_tensor(o_n[:, t % 2, :, :], o_sb[:, t % 2, :, 0:D],
                                            rms_f[:, t % 2, :].unsqueeze(2).broadcast_to([P, H, D]), ALU.mult)\
                        .then_inc(on_ready[0], 1)
                elif kind == "ot":
                    t = step[1]
                    reach(dve, ot_hi_ready, a, t + 1)
                    low(ot_lo[:, t % 2, :, :], att_bank(step)[:, 0:HG * P].rearrange("p (g n) -> p g n", g=HG),
                        ot_hi[:, t % 2, :, :]).then_inc(ot_ready[0], 1)
                elif kind == "ln2_stats":
                    p = step[1]
                    reach(dve, wo_copied, a, p + 1)
                    ln_stats(2, rows, range(2 * p, 2 * p + 2), bn2, mv2)
                elif kind == "ln2_add":
                    p = step[1]
                    ts = slice(2 * p, 2 * p + 2)
                    reach(dve, ln2_applied, a, p + 1)
                    reach(dve, x1_copied, a, 0)
                    nc.vector.tensor_tensor(x1[:, ts, :], rows[:, ts, :], xs[:, ts, :], ALU.add).then_inc(x1_ready[0], 1)
                elif kind == "ln3_stats":
                    p = step[1]
                    reach(dve, x1_ready, a, p + 1)
                    ln_stats(3, x1, range(2 * p, 2 * p + 2), bn3, mv3)
                elif kind == "ft_out":
                    p = step[1]
                    c = slice(p * 2 * P, (p + 1) * 2 * P)
                    reach(dve, ft_hi_ready, a, p + 1)
                    low(ft_lo[:, :, c], att_bank(("ft", p))[:, :].rearrange("p (k n) -> p k n", k=KT), ft_hi[:, :, c])\
                        .then_inc(ft_ready[0], 1)

            def hidden(e, m, f):
                reach(dve, silu_ready, f, 2 * e + m + 1)
                nc.vector.tensor_tensor(h_f[:, m, :], h_f[:, m, :], up_ps[m][:, :], ALU.mult).then_inc(h_ready[0], 1)

            def low_hidden(e, m, f):
                reach(dve, h_hi_ready, f, 2 * e + m + 1)
                low(h_lo[:, e % 2, m, :], h_f[:, m, :], h_hi[:, e % 2, m, :]).then_inc(h_lo_ready[0], 1)

            def add_down(e, p, f):
                if e == 0:
                    reach(dve, route_ready, f, 1)
                reach(dve, down_done, f, 2 * e + p + 1)
                for n in range(2):
                    t, src = 2 * p + n, down_ps[p][:, n * HID:(n + 1) * HID]
                    if e == 0:
                        last = nc.vector.tensor_scalar(acc[:, t, :], src, route[:, t, e:e + 1], None, ALU.mult)
                    else:
                        dst = fin if e == E - 1 else acc
                        last = nc.vector.scalar_tensor_tensor(dst[:, t, :], src, route[:, t, e:e + 1], acc[:, t, :],
                                                              ALU.mult, ALU.add)
                last.then_inc(down_read[0], 1)

            def out_stats(f):
                reach(dve, down_read, f, 2 * E)
                ln_stats(4, fin, range(TILES), bn4, mv4)

            def out_add(f):
                reach(dve, fin_ready, f, 1)
                reach(dve, x1_copied, f, 1)
                nc.vector.tensor_tensor(x1_kept[:, :, :], x1_kept[:, :, :], fin, ALU.add).then_inc(out_ready[0], 1)
                reach(dve, out_ready, f, 1)

            def route_rank(a):
                shape = [P, TILES, E, E]
                mine, other = (dist[:, :, :].unsqueeze(n).broadcast_to(shape) for n in (3, 2))
                reach(dve, dist_ready, a, 1)
                nc.vector.tensor_tensor(nearer[:, :, :, :], other, mine, ALU.is_lt)
                settle(nc.vector.tensor_tensor(as_near[:, :, :, :], other, mine, ALU.is_equal))
                settle(nc.vector.tensor_tensor(as_near[:, :, :, :], as_near[:, :, :, :],
                                               before[:, :, :, :].broadcast_to(shape), ALU.mult))
                settle(nc.vector.tensor_tensor(nearer[:, :, :, :], nearer[:, :, :, :], as_near[:, :, :, :], ALU.add))
                nc.vector.tensor_reduce(rank[:, :, :], nearer[:, :, :, :], AX.X, ALU.add).then_inc(rank_ready[0], 1)

            def route_weights(a):
                per_expert = [P, 2, TILES, E]
                reach(dve, rank_ready, a, 1)
                reach(dve, fallback_ready, a, 1)
                settle(nc.vector.tensor_tensor(cube[:, :, :], fallback[:, :, :], fallback[:, :, :], ALU.mult))
                nc.vector.scalar_tensor_tensor(kinds[:, 1, :, :], rank[:, :, :], 2.0, fallback[:, :, :], ALU.is_lt, ALU.mult)
                settle(nc.vector.tensor_tensor(cube[:, :, :], cube[:, :, :], fallback[:, :, :], ALU.mult))
                settle(nc.vector.tensor_tensor(kinds[:, 0, :, :], cube[:, :, :], zone[:, :, :], ALU.mult))
                settle(nc.vector.tensor_reduce(sums[:, :, :], kinds[:, :, :, :], AX.X, ALU.add))
                nc.vector.tensor_scalar(chosen[:, 0, :], sums[:, 0, :], TINY, None, ALU.is_ge)
                nc.vector.tensor_scalar(chosen[:, 1, :], sums[:, 0, :], TINY, None, ALU.is_lt)
                settle(nc.vector.tensor_scalar(guarded[:, :, :], sums[:, :, :], TINY, None, ALU.max))
                settle(nc.vector.reciprocal(guarded[:, :, :], guarded[:, :, :]))
                settle(nc.vector.tensor_tensor(guarded[:, :, :], guarded[:, :, :], chosen[:, :, :], ALU.mult))
                settle(nc.vector.tensor_tensor(kinds[:, :, :, :], kinds[:, :, :, :],
                                               guarded[:, :, :].unsqueeze(3).broadcast_to(per_expert), ALU.mult))
                nc.vector.tensor_tensor(route[:, :, :], kinds[:, 0, :, :], kinds[:, 1, :, :], ALU.add)\
                    .then_inc(route_ready[0], 1)

            def attention(n, a):
                for step in STEPS[n]:
                    att_step(step, a)

            def low_of_unit(u):
                dve.wait_ge(w_hi_ready, ATT_W + u + 1)
                low(w_lo[:, u, :, :], stage(u)[1], w_hi[:, u, :, :]).then_inc(w_ready, 1)

            x_stats((0, 0))
            for j in range(HPG):
                nc.vector.memset(kz[:, :, j, :], 0.0)
            nc.vector.memset(state[:, :, :, :], 0.0)
            settle(nc.vector.memset(v_sb[:, :, :, D:VA], 1.0))
            dve.wait_ge(small_loaded, 48)
            dve.wait_ge(att_w_loaded[2], 16)
            for g in range(HG):
                last = nc.vector.tensor_scalar(wo_raw[:, g, :], wo_raw[:, g, :], nw[:, g:g + 1], None, ALU.mult)
            last.then_inc(wo_scaled, 1)
            dve.wait_ge(w_hi_ready, 1)
            low(wq_lo[:, :, :], wq_raw, wq_hi[:, :, :]).then_inc(w_ready, 1)
            dve.wait_ge(w_hi_ready, 2)
            low(wkv_lo[:, :, :], wkv_raw, wkv_hi[:, :, :]).then_inc(w_ready, 1)
            dve.wait_ge(w_hi_ready, 3)
            low(wo_lo[:, :, :], wo_raw, wo_hi[:, :, :]).then_inc(w_ready, 1)
            dve.wait_ge(wr_hi_ready, 1)
            low(wr_hl[:, :, E:2 * E], wr_raw[:, :, :], wr_hl[:, :, 0:E]).then_inc(wr_ready, 1)
            settle(nc.vector.reciprocal(half_inv_t[:, :], temp[:, :]))
            nc.vector.tensor_scalar(half_inv_t[:, :], half_inv_t[:, :], 0.5, None, ALU.mult).then_inc(temp_ready, 1)
            dve.wait_ge(const_ready, 1)
            def first_expert(a, f, done):
                if a is not None:
                    attention(0, a)
                hidden(1, 0, f)
                low_hidden(1, 0, f)
                if done is not None:
                    out_stats(done)
                route_rank(f)
                route_weights(f)
                hidden(1, 1, f)
                low_hidden(1, 1, f)
                add_down(0, 0, f)
                add_down(0, 1, f)
                if done is not None:
                    out_add(done)

            def rest(a, f, more=True):
                for e in range(2, E - 1):
                    for m in range(MT):
                        hidden(e, m, f)
                        attention(4 * e - 4 + 2 * m, a)
                        low_hidden(e, m, f)
                        add_down(e - 1, m, f)
                        attention(4 * e - 3 + 2 * m, a)
                hidden(E - 1, 0, f)
                low_hidden(E - 1, 0, f)
                attention(4 * E - 8, a)
                attention(4 * E - 7, a)
                hidden(E - 1, 1, f)
                attention(4 * E - 6, a)
                low_hidden(E - 1, 1, f)
                attention(4 * E - 5, a)
                add_down(E - 2, 0, f)
                add_down(E - 2, 1, f)
                if more:
                    x_stats((a[0], a[1] + 1))
                for m in range(MT):
                    hidden(0, m, a)
                    low_hidden(0, m, a)
                    add_down(E - 1, m, f)

            for n in range(len(STEPS)):
                attention(n, (0, 0))
                if n < UNITS:
                    low_of_unit(n)
            x_stats((1, 0))
            for m in range(MT):
                hidden(0, m, (0, 0))
                low_hidden(0, m, (0, 0))
            first_expert((1, 0), (0, 0), None)
            with dve.Fori(1, BLOCKS - 1) as i:
                rest((i, 0), (i, -1))
                first_expert((i, 1), (i, 0), (i, -1))
            rest((BLOCKS - 1, 0), (BLOCKS - 2, 0), more=False)
            f = (BLOCKS - 1, 0)
            first_expert(None, f, (BLOCKS - 2, 0))
            for e in range(2, E):
                for m in range(MT):
                    hidden(e, m, f)
                    low_hidden(e, m, f)
                    add_down(e - 1, m, f)
            add_down(E - 1, 0, f)
            add_down(E - 1, 1, f)
            out_stats(f)
            out_add(f)

        @block_scope.gpsimd
        def _(pool):
            def settle(ins):
                ins.then_inc(pool_own, 1)
                pool.wait_ge(pool_own, 1).then_inc(pool_own, -1)

            def inverse_root(n, k, tiles, a, mv, var, rstd, shift):
                ones = minus_one[:, tiles]
                reach(pool, moments_ready[n - 1], a, k)
                nc.gpsimd.tensor_tensor(shift[:, tiles], mv[:, tiles, 0], ones, ALU.mult)
                settle(nc.gpsimd.tensor_scalar(var[:, tiles], mv[:, tiles, 1], LN_EPS, None, ALU.add))
                settle(nc.gpsimd.tensor_tensor(rstd[:, tiles], var[:, tiles], minus_half[:, tiles], ALU.pow))
                nc.gpsimd.tensor_tensor(shift[:, tiles], shift[:, tiles], rstd[:, tiles], ALU.mult)\
                    .then_inc(rstd_ready[n - 1][0], 1)

            def x_root(a):
                inverse_root(1, 1, slice(0, TILES), a, mv1, var1, rstd1, shift1)

            def out_root(f):
                inverse_root(4, 1, slice(0, TILES), f, mv4, var4, rstd4, shift4)

            def att_step(step, a):
                kind = step[0]
                if kind == "ln2_stats":
                    p = step[1]
                    inverse_root(2, p + 1, slice(2 * p, 2 * p + 2), a, mv2, var2, rstd2, shift2)
                elif kind == "ln3_stats":
                    p = step[1]
                    inverse_root(3, p + 1, slice(2 * p, 2 * p + 2), a, mv3, var3, rstd3, shift3)
                elif kind == "norm_stats":
                    t = step[1]
                    reach(pool, rms_in_ready, a, t + 1)
                    reach(pool, on_ready, a, t - 1)
                    nc.gpsimd.tensor_tensor(rms_f[:, t % 2, :], rms_in[:, :], minus_half[:, :], ALU.pow)\
                        .then_inc(rms_ready[0], 1)

            def router_logit(a):
                reach(pool, rz_copied, a, 1)
                nc.gpsimd.tensor_tensor(logit[:, :, :], rz[:, :, 0, :], rz[:, :, 1, :], ALU.add).then_inc(logit_ready[0], 1)

            def routing(a):
                reach(pool, tanh_ready, a, 1)
                settle(nc.gpsimd.tensor_tensor(inh[:, :, :], tanh[:, :, :],
                                               minus_one[:, :].unsqueeze(2).broadcast_to([P, TILES, E]), ALU.subtract))
                settle(nc.gpsimd.tensor_scalar(inh[:, :, :], inh[:, :, :], 0.5, None, ALU.mult))
                settle(nc.gpsimd.tensor_scalar(off[:, :, :], inh[:, :, :], CENTER, None, ALU.subtract))
                nc.gpsimd.tensor_scalar(neg_off[:, :, :], off[:, :, :], -1.0, 0.0, ALU.mult, ALU.max)
                settle(nc.gpsimd.tensor_scalar(off[:, :, :], off[:, :, :], 0.0, None, ALU.max))
                reach(pool, route_ready, a, 0)
                nc.gpsimd.tensor_tensor(dist[:, :, :], off[:, :, :], neg_off[:, :, :], ALU.add).then_inc(dist_ready[0], 1)
                nc.gpsimd.tensor_scalar(zone2[:, :, :], inh[:, :, :], UPPER, None, ALU.is_le)
                settle(nc.gpsimd.tensor_scalar(zone[:, :, :], inh[:, :, :], LOWER, None, ALU.is_ge))
                nc.gpsimd.tensor_tensor(zone[:, :, :], zone[:, :, :], zone2[:, :, :], ALU.mult)
                settle(nc.gpsimd.tensor_scalar(expo[:, :, :], dist[:, :, :], -1.0 / 0.3, None, ALU.mult))
                nc.gpsimd.tensor_tensor(fallback[:, :, :], euler[:, :, :], expo[:, :, :], ALU.pow)\
                    .then_inc(fallback_ready[0], 1)

            def attention(n, a):
                for step in STEPS[n]:
                    att_step(step, a)

            nc.gpsimd.memset(ident[:, :], 0.0)
            nc.gpsimd.memset(causal[:, :, :], 1.0)
            nc.gpsimd.memset(diag[:, :, :, :], 1.0)
            nc.gpsimd.memset(before[:, :, :, :], 1.0)
            nc.gpsimd.memset(minus_half[:, :], -0.5)
            nc.gpsimd.memset(minus_one[:, :], -1.0)
            settle(nc.gpsimd.memset(euler[:, :, :], math.e))
            nc.gpsimd.affine_select(out=ident[:, :], in_=ident[:, :], compare_op=ALU.not_equal, fill=1.0,
                                    base=0, pattern=[[-1, P]], channel_multiplier=1)
            nc.gpsimd.affine_select(out=causal[:, 0, :], in_=causal[:, 0, :], compare_op=ALU.is_ge, fill=0.0,
                                    base=0, pattern=[[1, P]], channel_multiplier=-1)
            nc.gpsimd.affine_select(out=before[:, 0, :, :], in_=before[:, 0, :, :], compare_op=ALU.is_ge, fill=0.0,
                                    base=-1, pattern=[[1, E], [-1, E]], channel_multiplier=0)
            settle(nc.gpsimd.affine_select(out=diag[:, 0, :, :], in_=diag[:, 0, :, :], compare_op=ALU.is_ge, fill=0.0,
                                           base=0, pattern=[[-D, HPG], [0, VA]], channel_multiplier=1))
            nc.gpsimd.affine_select(out=diag[:, 0, :, :], in_=diag[:, 0, :, :], compare_op=ALU.is_ge, fill=0.0,
                                    base=D - 1, pattern=[[D, HPG], [0, VA]], channel_multiplier=-1)\
                .then_inc(const_ready, 1)
            x_root((0, 0))
            for n in range(len(STEPS)):
                attention(n, (0, 0))
            router_logit((0, 0))
            x_root((1, 0))
            routing((0, 0))
            for n in range(4):
                attention(n, (1, 0))
            with pool.Fori(1, BLOCKS - 1) as i:
                for n in range(4, len(STEPS)):
                    attention(n, (i, 0))
                router_logit((i, 0))
                x_root((i, 1))
                routing((i, 0))
                out_root((i, -1))
                for n in range(4):
                    attention(n, (i, 1))
            for n in range(4, len(STEPS)):
                attention(n, (BLOCKS - 1, 0))
            router_logit((BLOCKS - 1, 0))
            routing((BLOCKS - 1, 0))
            out_root((BLOCKS - 2, 0))
            out_root((BLOCKS - 1, 0))


def kernel(L0_attn_hidden_states, L0_attn_Wq, L0_attn_Wk, L0_attn_Wv, L0_attn_Wo, L0_attn_norm_w,
           L0_ffn_Wg, L0_ffn_Wu, L0_ffn_Wd, L0_ffn_Wr, L0_ffn_temperature):
    import numpy as np
    import concourse.bacc as bacc
    from concourse import mybir as _mybir
    from concourse.bass_utils import run_bass_kernel_spmd

    layouts = {
        "x": L0_attn_hidden_states,
        "wq_t": np.transpose(L0_attn_Wq),
        "wkv_t": np.concatenate([np.transpose(L0_attn_Wk), np.transpose(L0_attn_Wv)], axis=1),
        "wo_t": np.transpose(L0_attn_Wo),
        "norm_w": np.tile(L0_attn_norm_w, H).reshape(HG, P).T,
        "wg": L0_ffn_Wg,
        "wu": L0_ffn_Wu,
        "wd": L0_ffn_Wd,
        "wr": L0_ffn_Wr,
        "temperature": L0_ffn_temperature,
    }
    nc = bacc.Bacc("TRN2", target_bir_lowering=False, num_devices=1)
    arrays, args = {}, []
    for name, a in layouts.items():
        a = np.ascontiguousarray(a)
        arrays[f"in_{name}"] = a
        args.append(nc.dram_tensor(f"in_{name}", a.shape, _mybir.dt.from_np(a.dtype), kind="ExternalInput").ap())
    args.append(nc.dram_tensor("out_rows", (B, S, HID), _mybir.dt.float32, kind="ExternalOutput").ap())
    build_program(nc, *args)
    result = run_bass_kernel_spmd(nc, [arrays], core_ids=[0])
    return result.results[0]["out_rows"]
```

```python
import math
from contextlib import ExitStack

import concourse.bass as bass
from concourse import mybir

B, S, HID = 2, 4096, 256
H, D = 8, 32
E, INNER = 8, 256
P = 128
KT = HID // P
HG = H * D // P
HPG = H // HG
MT = INNER // P
ROWS = 256
BLOCKS = S // ROWS
TILES = B * ROWS // P
TOK = TILES * P
VA = D + 1
GV = HPG * VA

LN_EPS = 1e-5
RMS_EPS = 1e-5
DENOM_EPS = 1.0
CENTER = 1.0 / math.e
LOWER = 0.5 - math.log(4.0 / 3.0)
UPPER = 0.5
TINY = 1e-8

STEPS = [
    [("xt", 0), ("xt", 1)],
    [("kv", 0), ("q", 0)],
    [("q", 1)],
    [("kt", 0), ("kv", 1)],
    [("s", 0, 0)],
    [("s", 0, 1), ("kt", 1)],
    [("o", 0), ("su", 0)],
    [("s", 1, 0), ("kv", 2), ("keep_x1",)],
    [("s", 1, 1), ("norm_stats", 0)],
    [("o", 1), ("su", 1), ("kt", 2), ("norm_apply", 0)],
    [("s", 2, 0), ("ot", 0)],
    [("s", 2, 1), ("norm_stats", 1), ("kv", 3)],
    [("o", 2), ("su", 2), ("kt", 3), ("norm_apply", 1)],
    [("s", 3, 0), ("ot", 1)],
    [("s", 3, 1), ("norm_stats", 2), ("wo", 0)],
    [("o", 3), ("su", 3), ("norm_apply", 2), ("ln2_stats", 0), ("norm_stats", 3)],
    [("ot", 2), ("ln2_apply", 0), ("norm_apply", 3)],
    [("ln2_add", 0), ("ln3_stats", 0)],
    [("ot", 3)],
    [("ln3_apply", 0)],
    [("wo", 1), ("ln2_stats", 1)],
    [("ln2_apply", 1)],
    [("ft", 0), ("ln2_add", 1), ("ln3_stats", 1)],
    [],
    [("ln3_apply", 1)],
    [("ft", 1)],
    [("ft_out", 0), ("ft_out", 1)],
    [],
]
FIRST_STEPS = [
    [("xt", 0), ("xt", 1)],
    [("kv", 0), ("q", 0)],
    [("q", 1), ("kt", 0)],
    [("kv", 1)],
    [("s", 0, 0), ("s", 0, 1)],
    [("kv", 2), ("kt", 1)],
    [("o", 0), ("su", 0), ("norm_stats", 0)],
    [("s", 1, 0), ("s", 1, 1)],
    [("kv", 3), ("kt", 2), ("norm_apply", 0)],
    [("o", 1), ("su", 1), ("norm_stats", 1)],
    [("s", 2, 0), ("s", 2, 1)],
    [("kt", 3), ("ot", 0), ("norm_apply", 1)],
    [("o", 2), ("su", 2), ("norm_stats", 2)],
    [("s", 3, 0), ("s", 3, 1)],
    [("ot", 1), ("norm_apply", 2)],
    [("o", 3), ("su", 3), ("norm_stats", 3)],
    [("wo", 0), ("ot", 2)],
    [("norm_apply", 3), ("ln2_stats", 0), ("ot", 3), ("ln2_apply", 0)],
    [("wo", 1), ("ln2_add", 0), ("ln3_stats", 0)],
    [("ln2_stats", 1), ("ln3_apply", 0)],
    [("ln2_apply", 1), ("ft", 0)],
    [("ln2_add", 1), ("ln3_stats", 1), ("ft_out", 0)],
    [("ln3_apply", 1)],
    [("ft", 1)],
    [("ft_out", 1)],
]
ROUTER = ("r",)


def psum_steps(steps):
    return [s for after in steps for s in after
            if s[0] in ("xt", "q", "kv", "kt", "s", "o", "su", "ot", "wo", "ft")] + [ROUTER]


PSUM_STEPS, FIRST_PSUM_STEPS = psum_steps(STEPS), psum_steps(FIRST_STEPS)
N_PSUM = len(PSUM_STEPS)


def build_program(nc, x, wq_t, wkv_t, wo_t, norm_w, wg, wu, wd, wr, temperature, out):
    f32, f32r = mybir.dt.float32, mybir.dt.float32r
    ALU, ACT, AX = mybir.AluOpType, mybir.ActivationFunctionType, mybir.AxisListType

    ctx = ExitStack()
    with ctx:
        def sb(name, shape, dt=f32):
            return ctx.enter_context(nc.sbuf_tensor(name, shape, dt))

        def sem(name):
            return ctx.enter_context(nc.semaphore(name))

        w_hi = sb("w_hi", [P, 3 * E, 2, 256], f32r)
        w_lo = sb("w_lo", [P, 3 * E, 2, 256], f32r)
        wq_hi, wq_lo = sb("wq_hi", [P, KT, HID], f32r), sb("wq_lo", [P, KT, HID], f32r)
        wkv_hi, wkv_lo = sb("wkv_hi", [P, KT, 2 * HID], f32r), sb("wkv_lo", [P, KT, 2 * HID], f32r)
        wo_hi, wo_lo = sb("wo_hi", [P, HG, HID], f32r), sb("wo_lo", [P, HG, HID], f32r)
        wr_raw = sb("wr_raw", [P, KT, E])
        wr_hl = sb("wr_hl", [P, KT, 2 * E], f32r)
        wr_h0 = sb("wr_h0", [P, KT, 2 * E], f32r)
        nw = sb("nw", [P, HG])
        temp = sb("temp", [P, 1])
        half_inv_t = sb("half_inv_t", [P, 1])

        xs = sb("xs", [P, TILES, HID])
        rows = sb("rows", [P, TILES, HID])
        xt_hi, xt_lo = sb("xt_hi", [P, KT, TOK], f32r), sb("xt_lo", [P, KT, TOK], f32r)
        q_t = sb("q_t", [P, HG, TOK])
        k_sb = sb("k_sb", [P, TILES, H * D])
        v_sb = sb("v_sb", [P, TILES, H, VA])
        kz = sb("kz", [P, HG, HPG, P])
        prob = sb("prob", [P, H, P])
        fin = prob[:, :, :].rearrange("p (t a) n -> p t (a n)", t=TILES)
        state = sb("state", [P, B, HG, GV])
        state_add = sb("state_add", [P, HG, GV])
        o_sb = sb("o_sb", [P, 2, H, VA])
        o_sq = sb("o_sq", [P, H, VA])
        o_n = sb("o_n", [P, 2, H, D])
        ot_hi, ot_lo = (xt[:, 0, :].rearrange("p (a g n) -> p a g n", a=2, g=HG) for xt in (xt_hi, xt_lo))
        x1 = sb("x1", [P, TILES, HID])

        ft_hi, ft_lo = sb("ft_hi", [P, KT, TOK], f32r), sb("ft_lo", [P, KT, TOK], f32r)
        h_hi, h_lo = sb("h_hi", [P, 2, MT, TOK], f32r), sb("h_lo", [P, 2, MT, TOK], f32r)
        NSTAGE = 6
        late = sb("late", [P, NSTAGE * 512])
        h_f = late[:, 0:1024].rearrange("p (m n) -> p m n", m=MT)
        acc = late[:, 1024:2048].rearrange("p (t n) -> p t n", t=TILES)
        x1_kept = late[:, 2048:3072].rearrange("p (t n) -> p t n", t=TILES)

        bn1, bn2, bn3, bn4 = (sb(f"bn{n}", [P, TILES, 6]) for n in (1, 2, 3, 4))
        mv1, mv2, mv3, mv4 = (sb(f"mv{n}", [P, TILES, 2]) for n in (1, 2, 3, 4))
        var1, var2, var3, var4 = (sb(f"var{n}", [P, TILES]) for n in (1, 2, 3, 4))
        rstd1, rstd2, rstd3, rstd4 = (sb(f"rstd{n}", [P, TILES]) for n in (1, 2, 3, 4))
        shift1, shift2, shift3, shift4 = (sb(f"shift{n}", [P, TILES]) for n in (1, 2, 3, 4))
        den2, ssq = sb("den2", [P, H]), sb("ssq", [P, H])
        rms_in, rms_f = sb("rms_in", [P, H]), sb("rms_f", [P, 2, H])
        ident = sb("ident", [P, P])
        causal = sb("causal", [P, 1, P])
        diag = sb("diag", [P, 1, HPG, VA])
        before = sb("before", [P, 1, E, E])
        minus_half, minus_one = sb("minus_half", [P, H]), sb("minus_one", [P, TILES])
        euler = sb("euler", [P, TILES, E])
        rz = sb("rz", [P, TILES, 2, E])
        logit, tanh, inh = (sb(n, [P, TILES, E]) for n in ("logit", "tanh", "inh"))
        off, neg_off, dist, zone, below = (sb(n, [P, TILES, E]) for n in ("off", "neg_off", "dist", "zone", "below"))
        expo, fallback, cube, rank = (sb(n, [P, TILES, E]) for n in ("expo", "fallback", "cube", "rank"))
        nearer, as_near = sb("nearer", [P, TILES, E, E]), sb("as_near", [P, TILES, E, E])
        kinds = sb("kinds", [P, 2, TILES, E])
        sums, guarded, chosen = (sb(n, [P, 2, TILES]) for n in ("sums", "guarded", "chosen"))
        route = sb("route", [P, TILES, E])

        def bank(name):
            return ctx.enter_context(nc.psum_tensor(name, [P, 512], f32))

        gate_ps = [bank(f"gate_ps{m}") for m in range(MT)]
        up_ps = [bank(f"up_ps{m}") for m in range(MT)]
        down_ps = [bank(f"down_ps{p}") for p in range(2)]
        att_ps = [bank(f"att_ps{n}") for n in range(2)]

        def counter(name, per_block, before_first=0):
            return sem(name), per_block, before_first

        x_loaded = counter("x_loaded", 32)
        out_stored = counter("out_stored", 32, 32)
        att_done = counter("att_done", N_PSUM)
        xn_ready = counter("xn_ready", 1)
        xt_hi_ready = counter("xt_hi_ready", KT)
        xt_ready = counter("xt_ready", KT)
        q_ready = counter("q_ready", HG)
        k_ready = counter("k_ready", TILES)
        v_ready = counter("v_ready", TILES)
        kz_ready = counter("kz_ready", TILES)
        prob_ready = counter("prob_ready", TILES * HG)
        o_copied = counter("o_copied", TILES)
        o_squared = counter("o_squared", TILES)
        rms_in_ready = counter("rms_in_ready", TILES)
        rms_ready = counter("rms_ready", TILES)
        on_ready = counter("on_ready", TILES)
        su_read = counter("su_read", TILES)
        state_ready = counter("state_ready", TILES)
        ot_hi_ready = counter("ot_hi_ready", TILES)
        ot_ready = counter("ot_ready", TILES)
        wo_copied = counter("wo_copied", 2)
        x1_ready = counter("x1_ready", 2)
        ln2_applied = counter("ln2_applied", 2)
        x1n_ready = counter("x1n_ready", 2)
        fin_ready = counter("fin_ready", 2)
        x1_copied = counter("x1_copied", 1)
        ft_hi_ready = counter("ft_hi_ready", 2)
        ft_ready = counter("ft_ready", 2)
        moments_ready = [counter(f"moments{n}_ready", k) for n, k in ((1, 1), (2, 2), (3, 2), (4, 2))]
        rstd_ready = [counter(f"rstd{n}_ready", k) for n, k in ((1, 1), (2, 2), (3, 2), (4, 2))]
        rz_copied = counter("rz_copied", 1)
        logit_ready = counter("logit_ready", 1)
        tanh_ready = counter("tanh_ready", 1)
        dist_ready = counter("dist_ready", 1)
        fallback_ready = counter("fallback_ready", 1)
        rank_ready = counter("rank_ready", 1)
        route_ready = counter("route_ready", 1)
        up_done = counter("up_done", 2 * E)
        silu_ready = counter("silu_ready", 2 * E)
        h_ready = counter("h_ready", 2 * E)
        h_hi_ready = counter("h_hi_ready", 2 * E)
        h_lo_ready = counter("h_lo_ready", 2 * E)
        down_done = counter("down_done", 2 * E)
        down_read = counter("down_read", 2 * E)
        out_ready = counter("out_ready", 2)
        att_w_loaded = [sem(f"att_w_loaded{n}") for n in range(3)]
        small_loaded = sem("small_loaded")
        stage_loaded = [sem(f"stage_loaded{n}") for n in range(NSTAGE)]
        w_hi_ready = sem("w_hi_ready")
        w_ready = sem("w_ready")
        wo_scaled = sem("wo_scaled")
        wr_hi_ready = sem("wr_hi_ready")
        wr_ready = sem("wr_ready")
        temp_ready = sem("temp_ready")
        const_ready = sem("const_ready")
        dve_own, pool_own = sem("dve_own"), sem("pool_own")

        def reach(eng, count, block, k):
            s, per_block, first = count
            base, offset = block
            value = offset * per_block + k + first
            if isinstance(base, int):
                if base * per_block + value > first:
                    eng.wait_ge(s, base * per_block + value)
            else:
                eng.wait_ge(s, base * per_block + value)

        READ_OUT = {ROUTER: (rz_copied, 1)}
        for n in range(KT):
            READ_OUT["xt", n] = (xt_ready, n + 1)
        for n in range(HG):
            READ_OUT["q", n] = (q_ready, n + 1)
        for t in range(TILES):
            READ_OUT["kv", t] = (v_ready, t + 1)
            READ_OUT["kt", t] = (kz_ready, t + 1)
            for g in range(HG):
                READ_OUT["s", t, g] = (prob_ready, HG * t + g + 1)
            READ_OUT["o", t] = (o_copied, t + 1)
            READ_OUT["su", t] = (su_read, t + 1)
            READ_OUT["ot", t] = (ot_ready, t + 1)
        for p in range(2):
            READ_OUT["wo", p] = (wo_copied, p + 1)
            READ_OUT["ft", p] = (ft_ready, p + 1)

        def psum_order(a):
            return FIRST_PSUM_STEPS if isinstance(a[0], int) and a[0] + a[1] == 0 else PSUM_STEPS

        def number_of(step, a):
            return psum_order(a).index(step)

        def att_bank(step, a):
            return att_ps[number_of(step, a) % 2]

        UNITS = 3 * E

        def unit_src(u):
            return (wg, wu, wd)[u % 3][u // 3, :, :].rearrange("(k p) n -> p k n", p=P)

        def stage(u):
            n = (u + 4) % NSTAGE
            return n, late[:, 512 * n:512 * n + 512].rearrange("p (k n) -> p k n", k=2)

        wq_raw = late[:, 0:512].rearrange("p (k n) -> p k n", k=KT)
        wkv_raw = late[:, 512:1536].rearrange("p (k n) -> p k n", k=KT)
        wo_raw = late[:, 1536:2048].rearrange("p (k n) -> p k n", k=HG)
        ATT_W = 3

        def rows_of(dram, b, row):
            return dram[b, bass.ds(row, ROWS), :].rearrange("(c p) n -> p c n", p=P)

        def tiles_of(tensor, b):
            return tensor[:, b:TILES:B, :]

        def out_add(engine, eng, p, f):
            ts = slice(2 * p, 2 * p + 2)
            reach(eng, x1_copied, f, 1)
            reach(eng, fin_ready, f, p + 1)
            engine.tensor_tensor(x1_kept[:, ts, :], x1_kept[:, ts, :], fin[:, ts, :], ALU.add).then_inc(out_ready[0], 1)

        block_scope = ctx.enter_context(nc.Block())

        @block_scope.sync
        def _(sp):
            def load_x(row):
                for b in range(B):
                    sp.dma_start(tiles_of(xs, b), rows_of(x, b, row)).then_inc(x_loaded[0], 16)

            def store_out(block, row):
                for p in range(2):
                    reach(sp, out_ready, block, p + 1)
                    sp.dma_start(out[:, bass.ds(row + p * P, P), :].rearrange("b p n -> p b n"),
                                 x1_kept[:, 2 * p:2 * p + 2, :]).then_inc(out_stored[0], 16)

            sp.sem_inc(out_stored[0], out_stored[2])
            load_x(0)
            sp.dma_start(wq_raw, wq_t.rearrange("(k p) n -> p k n", p=P)).then_inc(att_w_loaded[0], 16)
            sp.dma_start(wkv_raw, wkv_t.rearrange("(k p) n -> p k n", p=P)).then_inc(att_w_loaded[1], 16)
            sp.dma_start(nw[:, :], norm_w).then_inc(small_loaded, 16)
            sp.dma_start(wr_raw[:, :, :], wr.rearrange("(k p) n -> p k n", p=P)).then_inc(small_loaded, 16)
            sp.dma_start(temp[:, :], temperature.partition_broadcast(P)).then_inc(small_loaded, 16)
            sp.dma_start(wo_raw, wo_t.rearrange("(k p) n -> p k n", p=P)).then_inc(att_w_loaded[2], 16)
            for u in range(UNITS):
                n, slot = stage(u)
                if u >= 2:
                    sp.wait_ge(w_ready, {2: 1, 3: 2, 4: 2, 5: 3}.get(u, ATT_W + u - NSTAGE + 1))
                sp.dma_start(slot, unit_src(u)).then_inc(stage_loaded[n], 16)
            reach(sp, x1_ready, (0, 0), 2)
            load_x(ROWS)
            with sp.Fori(1, BLOCKS - 1) as i:
                reach(sp, x1_ready, (i, 0), 2)
                load_x(i * ROWS + ROWS)
                store_out((i, -1), i * ROWS - ROWS)
            store_out((BLOCKS - 2, 0), (BLOCKS - 2) * ROWS)
            store_out((BLOCKS - 1, 0), (BLOCKS - 1) * ROWS)
            reach(sp, out_stored, (BLOCKS, 0), 0)

        @block_scope.tensor
        def _(pe):
            def products(dst, pairs, before_low=None):
                terms = [(lhs, r_hi) for lhs_parts, (r_hi, _) in pairs for lhs in lhs_parts]
                low_terms = [(l_hi, r_lo) for (l_hi, _), (_, r_lo) in pairs]
                for n, (lhs, rhs) in enumerate(terms + low_terms):
                    if n == len(terms) and before_low:
                        before_low()
                    last = nc.tensor.matmul(dst, lhs, rhs, start=n == 0, stop=n == len(terms + low_terms) - 1)
                return last

            def att_step(step, a):
                if step not in PSUM_STEPS:
                    return
                kind, dst, number = step[0], att_bank(step, a), number_of(step, a)
                if number >= 2:
                    count, k = READ_OUT[psum_order(a)[number - 2]]
                    reach(pe, count, a, k)
                else:
                    count, k = READ_OUT[PSUM_STEPS[N_PSUM - 2 + (number + N_PSUM) % 2]]
                    reach(pe, count, (a[0], a[1] - 1), k)
                if kind == "xt":
                    k = step[1]
                    reach(pe, xn_ready, a, 1)
                    for t in range(TILES):
                        last = nc.tensor.transpose(dst[:, t * P:t * P + P], rows[:, t, k * P:k * P + P], ident[:, :])
                elif kind == "q":
                    g = step[1]
                    reach(pe, xt_ready, a, KT)
                    last = products(dst[:, :], [((wq_hi[:, k, g * P:g * P + P], wq_lo[:, k, g * P:g * P + P]),
                                                 (xt_hi[:, k, :], xt_lo[:, k, :])) for k in range(KT)])
                elif kind == "kv":
                    t = slice(step[1] * P, step[1] * P + P)
                    reach(pe, xt_ready, a, KT)
                    last = products(dst[:, :], [((xt_hi[:, k, t], xt_lo[:, k, t]), (wkv_hi[:, k, :], wkv_lo[:, k, :]))
                                                for k in range(KT)])
                elif kind == "kt":
                    t = step[1]
                    reach(pe, k_ready, a, t + 1)
                    for g in range(HG):
                        last = nc.tensor.transpose(dst[:, g * P:g * P + P], k_sb[:, t, g * P:g * P + P], ident[:, :])
                elif kind == "s":
                    t, g = step[1:]
                    reach(pe, q_ready, a, g + 1)
                    reach(pe, kz_ready, a, t + 1)
                    for j in range(HPG):
                        last = nc.tensor.matmul(dst[:, j * P:j * P + P], kz[:, g, j, :], q_t[:, g, t * P:t * P + P],
                                                start=True, stop=True)
                elif kind == "o":
                    t = step[1]
                    reach(pe, prob_ready, a, HG * t + HG)
                    reach(pe, v_ready, a, t + 1)
                    reach(pe, state_ready, a, t - B + 1)
                    for g in range(HG):
                        nc.tensor.matmul(dst[:, g * GV:g * GV + GV], q_t[:, g, t * P:t * P + P], state[:, t % B, g, :],
                                         start=True, stop=False)
                        for j in range(HPG):
                            h = g * HPG + j
                            last = nc.tensor.matmul(dst[:, h * VA:h * VA + VA], prob[:, h, :], v_sb[:, t, h, :],
                                                    start=False, stop=j == HPG - 1)
                elif kind == "su":
                    t = step[1]
                    for g in range(HG):
                        last = nc.tensor.matmul(dst[:, g * GV:g * GV + GV], k_sb[:, t, g * P:g * P + P],
                                                v_sb[:, t, g * HPG:g * HPG + HPG, :], start=True, stop=True)
                elif kind == "ot":
                    t = step[1]
                    reach(pe, on_ready, a, t + 1)
                    for g in range(HG):
                        last = nc.tensor.transpose(dst[:, g * P:g * P + P], o_n[:, t % 2, g * HPG:g * HPG + HPG, :],
                                                   ident[:, :])
                elif kind == "wo":
                    p = step[1]
                    reach(pe, ot_ready, a, 2 * p + 2)
                    for t in range(2):
                        last = products(dst[:, t * HID:t * HID + HID],
                                        [((ot_hi[:, t, g, :], ot_lo[:, t, g, :]), (wo_hi[:, g, :], wo_lo[:, g, :]))
                                         for g in range(HG)])
                elif kind == "ft":
                    p = step[1]
                    reach(pe, x1n_ready, a, p + 1)
                    for k in range(KT):
                        for t in range(2):
                            c = (2 * k + t) * P
                            last = nc.tensor.transpose(dst[:, c:c + P], rows[:, 2 * p + t, k * P:k * P + P], ident[:, :])
                elif kind == "r":
                    reach(pe, ft_ready, a, 2)
                    for t in range(TILES):
                        cols, ts = dst[:, t * 2 * E:(t + 1) * 2 * E], slice(t * P, t * P + P)
                        for k in range(KT):
                            nc.tensor.matmul(cols, ft_hi[:, k, ts], wr_hl[:, k, :], start=k == 0, stop=False)
                            last = nc.tensor.matmul(cols, ft_lo[:, k, ts], wr_h0[:, k, :], start=False, stop=k == KT - 1)
                last.then_inc(att_done[0], 1)

            def up(e, m, f):
                reach(pe, ft_hi_ready, f, 2)
                reach(pe, h_ready, f, 2 * e + m - 1)
                c = slice(m * P, m * P + P)
                for n, dst in ((0, gate_ps[m]), (1, up_ps[m])):
                    last = products(dst[:, :], [((w_hi[:, 3 * e + n, k, c], w_lo[:, 3 * e + n, k, c]),
                                                 (ft_hi[:, k, :], ft_lo[:, k, :])) for k in range(KT)],
                                    before_low=lambda: reach(pe, ft_ready, f, 2))
                last.then_inc(up_done[0], 1)

            def down(e, p, f):
                reach(pe, h_lo_ready, f, 2 * e + 2)
                reach(pe, down_read, f, 2 * e + p - 1)
                for t in range(2):
                    c = slice((2 * p + t) * P, (2 * p + t) * P + P)
                    last = products(down_ps[p][:, t * HID:t * HID + HID],
                                    [((h_hi[:, e % 2, m, c], h_lo[:, e % 2, m, c]),
                                      (w_hi[:, 3 * e + 2, m, :], w_lo[:, 3 * e + 2, m, :])) for m in range(MT)])
                last.then_inc(down_done[0], 1)

            def attention(n, a):
                for step in STEPS[n]:
                    att_step(step, a)

            def first_expert(a, f):
                attention(0, a)
                for m in range(MT):
                    up(1, m, f)
                    if m > 0:
                        attention(2 * m, a)
                    down(0, m, f)
                    attention(2 * m + 1, a)

            def rest(a, f):
                for e in range(2, E - 1):
                    for m in range(MT):
                        up(e, m, f)
                        attention(4 * e - 4 + 2 * m, a)
                        down(e - 1, m, f)
                        attention(4 * e - 3 + 2 * m, a)
                up(E - 1, 0, f)
                up(E - 1, 1, f)
                down(E - 2, 0, f)
                for n in range(4 * E - 8, 4 * E - 4):
                    attention(n, a)
                down(E - 2, 1, f)
                up(0, 0, a)
                att_step(ROUTER, a)
                down(E - 1, 0, f)
                up(0, 1, a)
                down(E - 1, 1, f)

            pe.wait_ge(const_ready, 1)
            for n, steps in enumerate(FIRST_STEPS):
                if n == 1:
                    pe.wait_ge(w_ready, ATT_W)
                for step in steps:
                    att_step(step, (0, 0))
            pe.wait_ge(w_ready, ATT_W + 3)
            up(0, 0, (0, 0))
            pe.wait_ge(wr_ready, 1)
            att_step(ROUTER, (0, 0))
            up(0, 1, (0, 0))
            pe.wait_ge(w_ready, ATT_W + UNITS)
            first_expert((1, 0), (0, 0))
            with pe.Fori(1, BLOCKS - 1) as i:
                rest((i, 0), (i, -1))
                first_expert((i, 1), (i, 0))
            rest((BLOCKS - 1, 0), (BLOCKS - 2, 0))
            f = (BLOCKS - 1, 0)
            for e in range(1, E):
                for m in range(MT):
                    up(e, m, f)
                    down(e - 1, m, f)
            down(E - 1, 0, f)
            down(E - 1, 1, f)

        @block_scope.scalar
        def _(act):
            def copy(dst, src):
                return nc.scalar.activation(dst, src, ACT.Copy)

            def ln_apply(n, k, a, dst, src, tiles, shift, rstd):
                reach(act, rstd_ready[n - 1], a, k)
                for t in tiles:
                    last = nc.scalar.activation(dst[:, t, :], src[:, t, :], ACT.Identity, bias=shift[:, t:t + 1],
                                                scale=rstd[:, t:t + 1])
                return last

            def normalise_x(a):
                ln_apply(1, 1, a, rows, xs, range(TILES), shift1, rstd1).then_inc(xn_ready[0], 1)

            def normalise_out(p, f):
                ln_apply(4, p + 1, f, fin, fin, range(2 * p, 2 * p + 2), shift4, rstd4).then_inc(fin_ready[0], 1)

            def att_step(step, a):
                kind = step[0]
                if step in PSUM_STEPS and kind not in ("s", "su", "ft"):
                    reach(act, att_done, a, number_of(step, a) + 1)
                    src = att_bank(step, a)
                if kind == "xt":
                    copy(xt_hi[:, step[1], :], src[:, :]).then_inc(xt_hi_ready[0], 1)
                elif kind == "q":
                    copy(q_t[:, step[1], :], src[:, :]).then_inc(q_ready[0], 1)
                elif kind == "kv":
                    t = step[1]
                    copy(k_sb[:, t, :], src[:, 0:HID]).then_inc(k_ready[0], 1)
                    copy(v_sb[:, t, :, 0:D], src[:, HID:2 * HID].rearrange("p (h d) -> p h d", h=H))\
                        .then_inc(v_ready[0], 1)
                elif kind == "kt":
                    for j in range(HPG):
                        r = slice(j * D, j * D + D)
                        last = copy(kz[r, :, j, :], src[r, 0:HG * P].rearrange("p (g s) -> p g s", g=HG))
                    last.then_inc(kz_ready[0], 1)
                elif kind == "o":
                    t = step[1]
                    reach(act, on_ready, a, t - 1)
                    copy(o_sb[:, t % 2, :, :], src[:, 0:H * VA].rearrange("p (h v) -> p h v", h=H))\
                        .then_inc(o_copied[0], 1)
                    reach(act, rms_in_ready, a, t)
                    reach(act, o_copied, a, t + 1)
                    nc.scalar.activation(o_sq[:, :, :], o_sb[:, t % 2, :, :], ACT.Square).then_inc(o_squared[0], 1)
                elif kind == "ot":
                    t = step[1]
                    copy(ot_hi[:, t % 2, :, :], src[:, 0:HG * P].rearrange("p (g n) -> p g n", g=HG))\
                        .then_inc(ot_hi_ready[0], 1)
                elif kind == "wo":
                    p = step[1]
                    copy(rows[:, 2 * p:2 * p + 2, :], src[:, :].rearrange("p (t n) -> p t n", t=2))\
                        .then_inc(wo_copied[0], 1)
                elif kind == "ft_out":
                    p = step[1]
                    reach(act, att_done, a, number_of(("ft", p), a) + 1)
                    reach(act, up_done, a, 0)
                    copy(ft_hi[:, :, p * 2 * P:(p + 1) * 2 * P], att_bank(("ft", p), a)[:, :].rearrange("p (k n) -> p k n", k=KT))\
                        .then_inc(ft_hi_ready[0], 1)
                elif kind == "ln2_apply":
                    p = step[1]
                    ln_apply(2, p + 1, a, rows, rows, range(2 * p, 2 * p + 2), shift2, rstd2).then_inc(ln2_applied[0], 1)
                elif kind == "ln3_apply":
                    p = step[1]
                    ln_apply(3, p + 1, a, rows, x1, range(2 * p, 2 * p + 2), shift3, rstd3).then_inc(x1n_ready[0], 1)
                elif kind == "r":
                    reach(act, logit_ready, a, 0)
                    copy(rz[:, :, :, :], src[:, 0:TILES * 2 * E].rearrange("p (t a e) -> p t a e", t=TILES, a=2))\
                        .then_inc(rz_copied[0], 1)

            def router_tanh(a):
                reach(act, logit_ready, a, 1)
                reach(act, dist_ready, a, 0)
                nc.scalar.activation(tanh[:, :, :], logit[:, :, :], ACT.Tanh, scale=half_inv_t[:, 0:1])\
                    .then_inc(tanh_ready[0], 1)

            def keep_x1(f):
                reach(act, x1_ready, f, 2)
                reach(act, out_stored, f, 0)
                copy(x1_kept[:, :, :], x1[:, :, :]).then_inc(x1_copied[0], 1)

            def silu(e, m, f):
                reach(act, up_done, f, 2 * e + m + 1)
                reach(act, h_lo_ready, f, 2 * e + m - 1)
                nc.scalar.activation(h_f[:, m, :], gate_ps[m][:, :], ACT.Silu).then_inc(silu_ready[0], 1)

            def high(e, m, f):
                reach(act, h_ready, f, 2 * e + m + 1)
                reach(act, down_done, f, 2 * e - 2)
                copy(h_hi[:, e % 2, m, :], h_f[:, m, :]).then_inc(h_hi_ready[0], 1)

            def attention(n, a, f=None):
                for step in STEPS[n]:
                    if step[0] == "keep_x1":
                        if f is not None:
                            keep_x1(f)
                    else:
                        att_step(step, a)

            def high_of_unit(u):
                n, raw = stage(u)
                act.wait_ge(stage_loaded[n], 16 * ((u // NSTAGE) + 1))
                copy(w_hi[:, u, :, :], raw).then_inc(w_hi_ready, 1)

            def first_expert(a, f, done):
                if a is not None:
                    attention(0, a, f)
                silu(1, 0, f)
                high(1, 0, f)
                if a is not None:
                    attention(1, a, f)
                if done is not None:
                    normalise_out(0, done)
                if a is not None:
                    attention(2, a, f)
                silu(1, 1, f)
                if done is not None:
                    normalise_out(1, done)
                high(1, 1, f)
                if a is not None:
                    attention(3, a, f)

            def rest(a, f, more=True):
                for e in range(2, E - 1):
                    for m in range(MT):
                        silu(e, m, f)
                        attention(4 * e - 4 + 2 * m, a, f)
                        high(e, m, f)
                        attention(4 * e - 3 + 2 * m, a, f)
                silu(E - 1, 0, f)
                high(E - 1, 0, f)
                attention(4 * E - 8, a, f)
                attention(4 * E - 7, a, f)
                silu(E - 1, 1, f)
                attention(4 * E - 6, a, f)
                high(E - 1, 1, f)
                attention(4 * E - 5, a, f)
                silu(0, 0, a)
                att_step(ROUTER, a)
                high(0, 0, a)
                if more:
                    normalise_x((a[0], a[1] + 1))
                silu(0, 1, a)
                router_tanh(a)
                high(0, 1, a)

            act.wait_ge(att_w_loaded[0], 16)
            copy(wq_hi[:, :, :], wq_raw).then_inc(w_hi_ready, 1)
            act.wait_ge(att_w_loaded[1], 16)
            copy(wkv_hi[:, :, :], wkv_raw).then_inc(w_hi_ready, 1)
            normalise_x((0, 0))
            act.wait_ge(wo_scaled, 1)
            copy(wo_hi[:, :, :], wo_raw).then_inc(w_hi_ready, 1)
            act.wait_ge(small_loaded, 48)
            copy(wr_hl[:, :, 0:E], wr_raw[:, :, :])
            copy(wr_h0[:, :, 0:E], wr_raw[:, :, :])
            nc.scalar.activation(wr_h0[:, :, E:2 * E], wr_raw[:, :, :], ACT.Copy, scale=0.0).then_inc(wr_hi_ready, 1)
            for n, steps in enumerate(FIRST_STEPS):
                for step in steps:
                    att_step(step, (0, 0))
                if n < UNITS:
                    high_of_unit(n)
            act.wait_ge(temp_ready, 1)
            act.wait_ge(w_ready, ATT_W + UNITS - 2)
            silu(0, 0, (0, 0))
            att_step(ROUTER, (0, 0))
            high(0, 0, (0, 0))
            router_tanh((0, 0))
            normalise_x((1, 0))
            silu(0, 1, (0, 0))
            high(0, 1, (0, 0))
            first_expert((1, 0), (0, 0), None)
            with act.Fori(1, BLOCKS - 1) as i:
                rest((i, 0), (i, -1))
                first_expert((i, 1), (i, 0), (i, -1))
            rest((BLOCKS - 1, 0), (BLOCKS - 2, 0), more=False)
            f = (BLOCKS - 1, 0)
            first_expert(None, f, (BLOCKS - 2, 0))
            keep_x1(f)
            for e in range(2, E):
                for m in range(MT):
                    silu(e, m, f)
                    high(e, m, f)
            normalise_out(0, f)
            normalise_out(1, f)

        @block_scope.vector
        def _(dve):
            def settle(ins):
                ins.then_inc(dve_own, 1)
                dve.wait_ge(dve_own, 1).then_inc(dve_own, -1)

            def low(dst, src, high_part):
                return nc.vector.tensor_tensor(dst, src, high_part.bitcast(f32), ALU.subtract)

            def ln_stats(n, src, tiles, bn, mv):
                for t in tiles:
                    last = nc.vector.bn_stats(bn[:, t, :], src[:, t, :])
                settle(last)
                for t in tiles:
                    last = nc.vector.bn_aggr(mv[:, t, :], bn[:, t, :])
                last.then_inc(moments_ready[n - 1][0], 1)

            def x_stats(a):
                reach(dve, x_loaded, a, 32)
                ln_stats(1, xs, range(TILES), bn1, mv1)

            def att_step(step, a):
                kind = step[0]
                if kind == "xt":
                    k = step[1]
                    reach(dve, xt_hi_ready, a, k + 1)
                    low(xt_lo[:, k, :], att_bank(step, a)[:, :], xt_hi[:, k, :]).then_inc(xt_ready[0], 1)
                elif kind == "s":
                    t, g = step[1:]
                    reach(dve, att_done, a, number_of(step, a) + 1)
                    nc.vector.tensor_tensor(prob[:, g * HPG:(g + 1) * HPG, :],
                                            att_bank(step, a)[:, :].rearrange("p (h n) -> p h n", h=HPG),
                                            causal[:, :, :].broadcast_to([P, HPG, P]), ALU.mult)\
                        .then_inc(prob_ready[0], 1)
                elif kind == "su":
                    t = step[1]
                    reach(dve, att_done, a, number_of(step, a) + 1)
                    nc.vector.tensor_tensor(state_add[:, :, :], att_bank(step, a)[:, 0:HG * GV].rearrange("p (g v) -> p g v", g=HG),
                                            diag[:, :, :, :].rearrange("p a j v -> p a (j v)").broadcast_to([P, HG, GV]),
                                            ALU.mult).then_inc(su_read[0], 1)
                    reach(dve, su_read, a, t + 1)
                    nc.vector.tensor_tensor(state[:, t % B, :, :], state[:, t % B, :, :], state_add[:, :, :], ALU.add)\
                        .then_inc(state_ready[0], 1)
                elif kind == "norm_stats":
                    t = step[1]
                    reach(dve, o_squared, a, t + 1)
                    nc.vector.tensor_scalar(den2[:, :], o_sq[:, :, D], DENOM_EPS ** 2, RMS_EPS, ALU.max, ALU.mult)
                    settle(nc.vector.tensor_reduce(ssq[:, :], o_sq[:, :, 0:D], AX.X, ALU.add))
                    nc.vector.scalar_tensor_tensor(rms_in[:, :], ssq[:, :], 1.0 / D, den2[:, :], ALU.mult, ALU.add)\
                        .then_inc(rms_in_ready[0], 1)
                elif kind == "norm_apply":
                    t = step[1]
                    reach(dve, rms_ready, a, t + 1)
                    if t >= 2:
                        reach(dve, att_done, a, number_of(("ot", t - 2), a) + 1)
                    nc.vector.tensor_tensor(o_n[:, t % 2, :, :], o_sb[:, t % 2, :, 0:D],
                                            rms_f[:, t % 2, :].unsqueeze(2).broadcast_to([P, H, D]), ALU.mult)\
                        .then_inc(on_ready[0], 1)
                elif kind == "ot":
                    t = step[1]
                    reach(dve, ot_hi_ready, a, t + 1)
                    low(ot_lo[:, t % 2, :, :], att_bank(step, a)[:, 0:HG * P].rearrange("p (g n) -> p g n", g=HG),
                        ot_hi[:, t % 2, :, :]).then_inc(ot_ready[0], 1)
                elif kind == "ln2_stats":
                    p = step[1]
                    reach(dve, wo_copied, a, p + 1)
                    ln_stats(2, rows, range(2 * p, 2 * p + 2), bn2, mv2)
                elif kind == "ln2_add":
                    p = step[1]
                    ts = slice(2 * p, 2 * p + 2)
                    reach(dve, ln2_applied, a, p + 1)
                    reach(dve, x1_copied, a, 0)
                    nc.vector.tensor_tensor(x1[:, ts, :], rows[:, ts, :], xs[:, ts, :], ALU.add).then_inc(x1_ready[0], 1)
                elif kind == "ln3_stats":
                    p = step[1]
                    reach(dve, x1_ready, a, p + 1)
                    ln_stats(3, x1, range(2 * p, 2 * p + 2), bn3, mv3)
                elif kind == "ft_out":
                    p = step[1]
                    c = slice(p * 2 * P, (p + 1) * 2 * P)
                    reach(dve, ft_hi_ready, a, p + 1)
                    low(ft_lo[:, :, c], att_bank(("ft", p), a)[:, :].rearrange("p (k n) -> p k n", k=KT), ft_hi[:, :, c])\
                        .then_inc(ft_ready[0], 1)

            def hidden(e, m, f):
                reach(dve, silu_ready, f, 2 * e + m + 1)
                nc.vector.tensor_tensor(h_f[:, m, :], h_f[:, m, :], up_ps[m][:, :], ALU.mult).then_inc(h_ready[0], 1)

            def low_hidden(e, m, f):
                reach(dve, h_hi_ready, f, 2 * e + m + 1)
                low(h_lo[:, e % 2, m, :], h_f[:, m, :], h_hi[:, e % 2, m, :]).then_inc(h_lo_ready[0], 1)

            def add_down(e, p, f):
                if e == 0:
                    reach(dve, route_ready, f, 1)
                reach(dve, down_done, f, 2 * e + p + 1)
                for n in range(2):
                    t, src = 2 * p + n, down_ps[p][:, n * HID:(n + 1) * HID]
                    if e == 0:
                        last = nc.vector.tensor_scalar(acc[:, t, :], src, route[:, t, e:e + 1], None, ALU.mult)
                    else:
                        dst = fin if e == E - 1 else acc
                        last = nc.vector.scalar_tensor_tensor(dst[:, t, :], src, route[:, t, e:e + 1], acc[:, t, :],
                                                              ALU.mult, ALU.add)
                last.then_inc(down_read[0], 1)

            def out_stats(p, f):
                reach(dve, down_read, f, 2 * E - 1 + p)
                ln_stats(4, fin, range(2 * p, 2 * p + 2), bn4, mv4)

            def route_rank(a):
                shape = [P, TILES, E, E]
                mine, other = (dist[:, :, :].unsqueeze(n).broadcast_to(shape) for n in (3, 2))
                reach(dve, dist_ready, a, 1)
                nc.vector.tensor_tensor(nearer[:, :, :, :], other, mine, ALU.is_lt)
                settle(nc.vector.tensor_tensor(as_near[:, :, :, :], other, mine, ALU.is_equal))
                settle(nc.vector.tensor_tensor(as_near[:, :, :, :], as_near[:, :, :, :],
                                               before[:, :, :, :].broadcast_to(shape), ALU.mult))
                settle(nc.vector.tensor_tensor(nearer[:, :, :, :], nearer[:, :, :, :], as_near[:, :, :, :], ALU.add))
                nc.vector.tensor_reduce(rank[:, :, :], nearer[:, :, :, :], AX.X, ALU.add).then_inc(rank_ready[0], 1)

            def route_weights(a):
                per_expert = [P, 2, TILES, E]
                reach(dve, rank_ready, a, 1)
                reach(dve, fallback_ready, a, 1)
                settle(nc.vector.tensor_tensor(cube[:, :, :], fallback[:, :, :], fallback[:, :, :], ALU.mult))
                nc.vector.scalar_tensor_tensor(kinds[:, 1, :, :], rank[:, :, :], 2.0, fallback[:, :, :], ALU.is_lt, ALU.mult)
                settle(nc.vector.tensor_tensor(cube[:, :, :], cube[:, :, :], fallback[:, :, :], ALU.mult))
                settle(nc.vector.tensor_tensor(kinds[:, 0, :, :], cube[:, :, :], zone[:, :, :], ALU.mult))
                settle(nc.vector.tensor_reduce(sums[:, :, :], kinds[:, :, :, :], AX.X, ALU.add))
                nc.vector.tensor_scalar(chosen[:, 0, :], sums[:, 0, :], TINY, None, ALU.is_ge)
                nc.vector.tensor_scalar(chosen[:, 1, :], sums[:, 0, :], TINY, None, ALU.is_lt)
                settle(nc.vector.tensor_scalar(guarded[:, :, :], sums[:, :, :], TINY, None, ALU.max))
                settle(nc.vector.reciprocal(guarded[:, :, :], guarded[:, :, :]))
                settle(nc.vector.tensor_tensor(guarded[:, :, :], guarded[:, :, :], chosen[:, :, :], ALU.mult))
                settle(nc.vector.tensor_tensor(kinds[:, :, :, :], kinds[:, :, :, :],
                                               guarded[:, :, :].unsqueeze(3).broadcast_to(per_expert), ALU.mult))
                nc.vector.tensor_tensor(route[:, :, :], kinds[:, 0, :, :], kinds[:, 1, :, :], ALU.add)\
                    .then_inc(route_ready[0], 1)

            def attention(n, a):
                for step in STEPS[n]:
                    att_step(step, a)

            LAG = 2

            def low_of_unit(u):
                dve.wait_ge(w_hi_ready, ATT_W + u + 1)
                low(w_lo[:, u, :, :], stage(u)[1], w_hi[:, u, :, :]).then_inc(w_ready, 1)

            x_stats((0, 0))
            for j in range(HPG):
                nc.vector.memset(kz[:, :, j, :], 0.0)
            nc.vector.memset(state[:, :, :, :], 0.0)
            settle(nc.vector.memset(v_sb[:, :, :, D:VA], 1.0))
            dve.wait_ge(small_loaded, 48)
            dve.wait_ge(att_w_loaded[2], 16)
            for g in range(HG):
                last = nc.vector.tensor_scalar(wo_raw[:, g, :], wo_raw[:, g, :], nw[:, g:g + 1], None, ALU.mult)
            last.then_inc(wo_scaled, 1)
            dve.wait_ge(w_hi_ready, 1)
            low(wq_lo[:, :, :], wq_raw, wq_hi[:, :, :]).then_inc(w_ready, 1)
            dve.wait_ge(w_hi_ready, 2)
            low(wkv_lo[:, :, :], wkv_raw, wkv_hi[:, :, :]).then_inc(w_ready, 1)
            dve.wait_ge(w_hi_ready, 3)
            low(wo_lo[:, :, :], wo_raw, wo_hi[:, :, :]).then_inc(w_ready, 1)
            dve.wait_ge(wr_hi_ready, 1)
            low(wr_hl[:, :, E:2 * E], wr_raw[:, :, :], wr_hl[:, :, 0:E]).then_inc(wr_ready, 1)
            settle(nc.vector.reciprocal(half_inv_t[:, :], temp[:, :]))
            nc.vector.tensor_scalar(half_inv_t[:, :], half_inv_t[:, :], 0.5, None, ALU.mult).then_inc(temp_ready, 1)
            dve.wait_ge(const_ready, 1)

            def first_expert(a, f, done):
                if a is not None:
                    attention(0, a)
                hidden(1, 0, f)
                low_hidden(1, 0, f)
                if done is not None:
                    out_stats(0, done)
                    out_stats(1, done)
                route_rank(f)
                route_weights(f)
                hidden(1, 1, f)
                low_hidden(1, 1, f)
                add_down(0, 0, f)
                add_down(0, 1, f)
                if done is not None:
                    reach(dve, out_ready, done, 2)

            def rest(a, f, more=True):
                for e in range(2, E - 1):
                    for m in range(MT):
                        hidden(e, m, f)
                        attention(4 * e - 4 + 2 * m, a)
                        low_hidden(e, m, f)
                        add_down(e - 1, m, f)
                        attention(4 * e - 3 + 2 * m, a)
                hidden(E - 1, 0, f)
                low_hidden(E - 1, 0, f)
                attention(4 * E - 8, a)
                attention(4 * E - 7, a)
                hidden(E - 1, 1, f)
                attention(4 * E - 6, a)
                low_hidden(E - 1, 1, f)
                attention(4 * E - 5, a)
                add_down(E - 2, 0, f)
                add_down(E - 2, 1, f)
                if more:
                    x_stats((a[0], a[1] + 1))
                for m in range(MT):
                    hidden(0, m, a)
                    low_hidden(0, m, a)
                    add_down(E - 1, m, f)

            for n, steps in enumerate(FIRST_STEPS):
                for step in steps:
                    att_step(step, (0, 0))
                if n >= LAG:
                    low_of_unit(n - LAG)
            for u in range(len(FIRST_STEPS) - LAG, UNITS):
                low_of_unit(u)
            x_stats((1, 0))
            for m in range(MT):
                hidden(0, m, (0, 0))
                low_hidden(0, m, (0, 0))
            first_expert((1, 0), (0, 0), None)
            with dve.Fori(1, BLOCKS - 1) as i:
                rest((i, 0), (i, -1))
                first_expert((i, 1), (i, 0), (i, -1))
            rest((BLOCKS - 1, 0), (BLOCKS - 2, 0), more=False)
            f = (BLOCKS - 1, 0)
            first_expert(None, f, (BLOCKS - 2, 0))
            for e in range(2, E):
                for m in range(MT):
                    hidden(e, m, f)
                    low_hidden(e, m, f)
                    add_down(e - 1, m, f)
            for p in range(2):
                add_down(E - 1, p, f)
                out_stats(p, f)
            for p in range(2):
                out_add(nc.vector, dve, p, f)

        @block_scope.gpsimd
        def _(pool):
            def settle(ins):
                ins.then_inc(pool_own, 1)
                pool.wait_ge(pool_own, 1).then_inc(pool_own, -1)

            def inverse_root(n, k, tiles, a, mv, var, rstd, shift):
                reach(pool, moments_ready[n - 1], a, k)
                nc.gpsimd.tensor_tensor(shift[:, tiles], mv[:, tiles, 0], minus_one[:, tiles], ALU.mult)
                settle(nc.gpsimd.tensor_scalar(var[:, tiles], mv[:, tiles, 1], LN_EPS, None, ALU.add))
                settle(nc.gpsimd.tensor_tensor(rstd[:, tiles], var[:, tiles], minus_half[:, tiles], ALU.pow))
                nc.gpsimd.tensor_tensor(shift[:, tiles], shift[:, tiles], rstd[:, tiles], ALU.mult)\
                    .then_inc(rstd_ready[n - 1][0], 1)

            def x_root(a):
                inverse_root(1, 1, slice(0, TILES), a, mv1, var1, rstd1, shift1)

            def out_root(f):
                for p in range(2):
                    inverse_root(4, p + 1, slice(2 * p, 2 * p + 2), f, mv4, var4, rstd4, shift4)

            def att_step(step, a):
                kind = step[0]
                if kind == "ln2_stats":
                    p = step[1]
                    inverse_root(2, p + 1, slice(2 * p, 2 * p + 2), a, mv2, var2, rstd2, shift2)
                elif kind == "ln3_stats":
                    p = step[1]
                    inverse_root(3, p + 1, slice(2 * p, 2 * p + 2), a, mv3, var3, rstd3, shift3)
                elif kind == "norm_stats":
                    t = step[1]
                    reach(pool, rms_in_ready, a, t + 1)
                    reach(pool, on_ready, a, t - 1)
                    nc.gpsimd.tensor_tensor(rms_f[:, t % 2, :], rms_in[:, :], minus_half[:, :], ALU.pow)\
                        .then_inc(rms_ready[0], 1)

            def router_logit(a):
                reach(pool, rz_copied, a, 1)
                nc.gpsimd.tensor_tensor(logit[:, :, :], rz[:, :, 0, :], rz[:, :, 1, :], ALU.add).then_inc(logit_ready[0], 1)

            def routing(a):
                reach(pool, tanh_ready, a, 1)
                settle(nc.gpsimd.tensor_tensor(inh[:, :, :], tanh[:, :, :],
                                               minus_one[:, :].unsqueeze(2).broadcast_to([P, TILES, E]), ALU.subtract))
                settle(nc.gpsimd.tensor_scalar(inh[:, :, :], inh[:, :, :], 0.5, None, ALU.mult))
                settle(nc.gpsimd.tensor_scalar(off[:, :, :], inh[:, :, :], CENTER, None, ALU.subtract))
                nc.gpsimd.tensor_scalar(neg_off[:, :, :], off[:, :, :], -1.0, 0.0, ALU.mult, ALU.max)
                settle(nc.gpsimd.tensor_scalar(off[:, :, :], off[:, :, :], 0.0, None, ALU.max))
                reach(pool, route_ready, a, 0)
                nc.gpsimd.tensor_tensor(dist[:, :, :], off[:, :, :], neg_off[:, :, :], ALU.add).then_inc(dist_ready[0], 1)
                nc.gpsimd.tensor_scalar(below[:, :, :], inh[:, :, :], UPPER, None, ALU.is_le)
                settle(nc.gpsimd.tensor_scalar(zone[:, :, :], inh[:, :, :], LOWER, None, ALU.is_ge))
                nc.gpsimd.tensor_tensor(zone[:, :, :], zone[:, :, :], below[:, :, :], ALU.mult)
                settle(nc.gpsimd.tensor_scalar(expo[:, :, :], dist[:, :, :], -1.0 / 0.3, None, ALU.mult))
                nc.gpsimd.tensor_tensor(fallback[:, :, :], euler[:, :, :], expo[:, :, :], ALU.pow)\
                    .then_inc(fallback_ready[0], 1)

            def attention(n, a):
                for step in STEPS[n]:
                    att_step(step, a)

            nc.gpsimd.memset(ident[:, :], 0.0)
            nc.gpsimd.memset(causal[:, :, :], 1.0)
            nc.gpsimd.memset(diag[:, :, :, :], 1.0)
            nc.gpsimd.memset(before[:, :, :, :], 1.0)
            nc.gpsimd.memset(minus_half[:, :], -0.5)
            nc.gpsimd.memset(minus_one[:, :], -1.0)
            settle(nc.gpsimd.memset(euler[:, :, :], math.e))
            nc.gpsimd.affine_select(out=ident[:, :], in_=ident[:, :], compare_op=ALU.not_equal, fill=1.0,
                                    base=0, pattern=[[-1, P]], channel_multiplier=1)
            nc.gpsimd.affine_select(out=causal[:, 0, :], in_=causal[:, 0, :], compare_op=ALU.is_ge, fill=0.0,
                                    base=0, pattern=[[1, P]], channel_multiplier=-1)
            nc.gpsimd.affine_select(out=before[:, 0, :, :], in_=before[:, 0, :, :], compare_op=ALU.is_ge, fill=0.0,
                                    base=-1, pattern=[[1, E], [-1, E]], channel_multiplier=0)
            settle(nc.gpsimd.affine_select(out=diag[:, 0, :, :], in_=diag[:, 0, :, :], compare_op=ALU.is_ge, fill=0.0,
                                           base=0, pattern=[[-D, HPG], [0, VA]], channel_multiplier=1))
            nc.gpsimd.affine_select(out=diag[:, 0, :, :], in_=diag[:, 0, :, :], compare_op=ALU.is_ge, fill=0.0,
                                    base=D - 1, pattern=[[D, HPG], [0, VA]], channel_multiplier=-1)\
                .then_inc(const_ready, 1)
            x_root((0, 0))
            for steps in FIRST_STEPS:
                for step in steps:
                    att_step(step, (0, 0))
            router_logit((0, 0))
            x_root((1, 0))
            routing((0, 0))
            for n in range(4):
                attention(n, (1, 0))
            with pool.Fori(1, BLOCKS - 1) as i:
                for n in range(4, len(STEPS)):
                    attention(n, (i, 0))
                x_root((i, 1))
                router_logit((i, 0))
                routing((i, 0))
                out_root((i, -1))
                for p in range(2):
                    out_add(nc.gpsimd, pool, p, (i, -1))
                for n in range(4):
                    attention(n, (i, 1))
            for n in range(4, len(STEPS)):
                attention(n, (BLOCKS - 1, 0))
            router_logit((BLOCKS - 1, 0))
            routing((BLOCKS - 1, 0))
            out_root((BLOCKS - 2, 0))
            for p in range(2):
                out_add(nc.gpsimd, pool, p, (BLOCKS - 2, 0))
            out_root((BLOCKS - 1, 0))


def kernel(L0_attn_hidden_states, L0_attn_Wq, L0_attn_Wk, L0_attn_Wv, L0_attn_Wo, L0_attn_norm_w,
           L0_ffn_Wg, L0_ffn_Wu, L0_ffn_Wd, L0_ffn_Wr, L0_ffn_temperature):
    import numpy as np
    import concourse.bacc as bacc
    from concourse import mybir as _mybir
    from concourse.bass_utils import run_bass_kernel_spmd

    layouts = {
        "x": L0_attn_hidden_states,
        "wq_t": np.transpose(L0_attn_Wq),
        "wkv_t": np.concatenate([np.transpose(L0_attn_Wk), np.transpose(L0_attn_Wv)], axis=1),
        "wo_t": np.transpose(L0_attn_Wo),
        "norm_w": np.tile(L0_attn_norm_w, H).reshape(HG, P).T,
        "wg": L0_ffn_Wg,
        "wu": L0_ffn_Wu,
        "wd": L0_ffn_Wd,
        "wr": L0_ffn_Wr,
        "temperature": L0_ffn_temperature,
    }
    nc = bacc.Bacc("TRN2", target_bir_lowering=False, num_devices=1)
    arrays, args = {}, []
    for name, a in layouts.items():
        a = np.ascontiguousarray(a)
        arrays[f"in_{name}"] = a
        args.append(nc.dram_tensor(f"in_{name}", a.shape, _mybir.dt.from_np(a.dtype), kind="ExternalInput").ap())
    args.append(nc.dram_tensor("out_rows", (B, S, HID), _mybir.dt.float32, kind="ExternalOutput").ap())
    build_program(nc, *args)
    result = run_bass_kernel_spmd(nc, [arrays], core_ids=[0])
    return result.results[0]["out_rows"]
```
